# Optimizing a Trainium2 kernel written in Bass

```python
import numpy as np
import jax
import jax.numpy as jnp

def _softmax(x, axis=-1):
    return jax.nn.softmax(x, axis=axis)
def _gelu(x):
    return jax.nn.gelu(x, approximate=True)
def _silu(x):
    return jax.nn.silu(x)
def _sigmoid(x):
    return jax.nn.sigmoid(x)
def _layernorm(x, axis=-1, eps=1e-5):
    m = jnp.mean(x, axis=axis, keepdims=True)
    v = jnp.var(x, axis=axis, keepdims=True)
    return (x - m) / jnp.sqrt(v + eps)
def _scatter_add(tgt, idx, src, axis=0):
    return tgt.at[idx].add(src)
def _segment_sum(src, seg, n):
    return jax.ops.segment_sum(src, seg, n)

kernel_name = 'mk_conv_preact_d2_conv_nchw128_b36e5a'

def setup_inputs(seed: int = 0):
    np.random.seed(seed)
    _w = jnp.asarray
    def _rec_inputs():
        import jax
        import jax.numpy as jnp
        _gk = jax.random.key(seed)
        x = -0.0003929 + 0.9999 * jax.random.normal(jax.random.fold_in(_gk, 1), (2, 128, 256, 256), jnp.float32)
        return x
    x = _rec_inputs()
    def _L0_conv_setup():
        import jax, jax.numpy as jnp
        import numpy as np
        DIM = 128
        WS = 8
        OWS = int(WS * 0.5) + WS
        HEADS = 4
        DH = 32
        INNER = HEADS * DH
        SCALE = DH ** (-0.5)
        PAD = (OWS - WS) // 2

        def fixed_pos_mask():
            size = WS + OWS - 1
            table = np.zeros((size, size), dtype=np.float32)
            table[0::2, :] = -np.inf
            table[:, 0::2] = -np.inf
            table = table.reshape(-1)
            c1 = np.stack(np.meshgrid(np.arange(WS), np.arange(WS), indexing='ij')).reshape(2, -1)
            c2 = np.stack(np.meshgrid(np.arange(OWS), np.arange(OWS), indexing='ij')).reshape(2, -1)
            rel = (c1[:, :, None] - c2[:, None, :]).transpose(1, 2, 0)
            rel[..., 0] += OWS - 1
            rel[..., 1] += OWS - 1
            rel[..., 0] *= size
            idx = rel.sum(-1)
            return jnp.asarray(table[idx.reshape(-1)].reshape(1, WS * WS, OWS * OWS))
        FIXED_MASK = fixed_pos_mask()

        def rel_to_abs(x):
            b, l, m = x.shape
            r = (m + 1) // 2
            x = jnp.pad(x, ((0, 0), (0, 0), (0, 1))).reshape(b, l * (m + 1))
            x = jnp.pad(x, ((0, 0), (0, m - l))).reshape(b, l + 1, m)
            return x[:, :l, -r:]

        def relative_logits_1d(q, rel_k):
            b, h, w, _ = q.shape
            r = (rel_k.shape[0] + 1) // 2
            logits = jnp.einsum('bxyd,rd->bxyr', q, rel_k)
            logits = rel_to_abs(logits.reshape(b * h, w, 2 * r - 1)).reshape(b, h, w, r)
            return jnp.broadcast_to(logits[:, :, None, :, :], (b, h, r, w, r))

        def rel_pos_emb(q, rel_height, rel_width):
            b = q.shape[0]
            q2 = q.reshape(b, WS, WS, DH)
            lw = relative_logits_1d(q2, rel_width)
            lw = lw.transpose(0, 1, 3, 2, 4).reshape(b, WS * WS, OWS * OWS)
            lh = relative_logits_1d(q2.transpose(0, 2, 1, 3), rel_height)
            lh = lh.transpose(0, 3, 1, 4, 2).reshape(b, WS * WS, OWS * OWS)
            return lw + lh

        def unfold_windows(x):
            b, c, H, W = x.shape
            xp = jnp.pad(x, ((0, 0), (0, 0), (PAD, PAD), (PAD, PAD)))
            nW = (H + 2 * PAD - OWS) // WS + 1
            idx = (jnp.arange(nW) * WS)[:, None] + jnp.arange(OWS)[None, :]
            w = xp[:, :, idx[:, :, None, None], idx[None, None, :, :]]
            w = w.transpose(0, 2, 4, 3, 5, 1)
            return w.reshape(b * nW * nW, OWS * OWS, c)

        def split_heads(t):
            B, n, _ = t.shape
            return t.reshape(B, n, HEADS, DH).transpose(0, 2, 1, 3).reshape(B * HEADS, n, DH)
        key = jax.random.key(seed)
        ks = jax.random.split(key, 5)
        x = jax.random.normal(ks[0], (2, DIM, 256, 256), jnp.float32)
        W_qkv = jax.random.normal(ks[1], (3 * INNER, DIM), jnp.float32) * DIM ** (-0.5)
        W_out = jax.random.normal(ks[2], (DIM, INNER), jnp.float32) * INNER ** (-0.5)
        rel_height = jax.random.normal(ks[3], (2 * OWS - 1, DH), jnp.float32) * SCALE
        rel_width = jax.random.normal(ks[4], (2 * OWS - 1, DH), jnp.float32) * SCALE
        return {'x': x, 'W_qkv': W_qkv, 'W_out': W_out, 'rel_height': rel_height, 'rel_width': rel_width}
    _L0_conv_all = _L0_conv_setup()
    _L0_conv_in = {k: v for k, v in _L0_conv_all.items() if k in ('W_qkv', 'W_out', 'rel_height', 'rel_width', )}
    del _L0_conv_all

    def _L1_conv_setup():
        import jax, jax.numpy as jnp
        import numpy as np
        TILE = 32
        THRESHOLD = 1e-06

        def _tile_mask(x):
            N, C, H, W = x.shape
            xb = jnp.abs(x).reshape(N, C, H // TILE, TILE, W // TILE, TILE)
            active = xb.max(axis=(1, 3, 5)) > THRESHOLD
            m = jnp.repeat(jnp.repeat(active, TILE, axis=1), TILE, axis=2)
            return m[:, None, :, :].astype(x.dtype)
        key = jax.random.key(seed)
        k_x, k_w, k_b = jax.random.split(key, 3)
        C_IN, C_OUT, K = (128, 128, 3)
        x = jax.random.normal(k_x, (16, C_IN, 128, 128), dtype=jnp.float32)
        fan_in = C_IN * K * K
        bw = 1.0 / np.sqrt(fan_in)
        weight = jax.random.uniform(k_w, (C_OUT, C_IN, K, K), dtype=jnp.float32, minval=-bw, maxval=bw)
        bias = jax.random.uniform(k_b, (C_OUT,), dtype=jnp.float32, minval=-bw, maxval=bw)
        return {'x': x, 'weight': weight, 'bias': bias}
    _L1_conv_all = _L1_conv_setup()
    _L1_conv_in = {k: v for k, v in _L1_conv_all.items() if k in ('weight', 'bias', )}
    del _L1_conv_all

    return {
        "x": x,
        "L0_conv_W_qkv": _L0_conv_in["W_qkv"],
        "L0_conv_W_out": _L0_conv_in["W_out"],
        "L0_conv_rel_height": _L0_conv_in["rel_height"],
        "L0_conv_rel_width": _L0_conv_in["rel_width"],
        "L1_conv_weight": _L1_conv_in["weight"],
        "L1_conv_bias": _L1_conv_in["bias"],
    }

def reference(x, L0_conv_W_qkv, L0_conv_W_out, L0_conv_rel_height, L0_conv_rel_width, L1_conv_weight, L1_conv_bias):
    import jax
    import jax.numpy as jnp
    def _L0_conv_ref(x, W_qkv, W_out, rel_height, rel_width):
        import jax, jax.numpy as jnp
        import numpy as np
        DIM = 128
        WS = 8
        OWS = int(WS * 0.5) + WS
        HEADS = 4
        DH = 32
        INNER = HEADS * DH
        SCALE = DH ** (-0.5)
        PAD = (OWS - WS) // 2

        def fixed_pos_mask():
            size = WS + OWS - 1
            table = np.zeros((size, size), dtype=np.float32)
            table[0::2, :] = -np.inf
            table[:, 0::2] = -np.inf
            table = table.reshape(-1)
            c1 = np.stack(np.meshgrid(np.arange(WS), np.arange(WS), indexing='ij')).reshape(2, -1)
            c2 = np.stack(np.meshgrid(np.arange(OWS), np.arange(OWS), indexing='ij')).reshape(2, -1)
            rel = (c1[:, :, None] - c2[:, None, :]).transpose(1, 2, 0)
            rel[..., 0] += OWS - 1
            rel[..., 1] += OWS - 1
            rel[..., 0] *= size
            idx = rel.sum(-1)
            return jnp.asarray(table[idx.reshape(-1)].reshape(1, WS * WS, OWS * OWS))
        FIXED_MASK = fixed_pos_mask()

        def rel_to_abs(x):
            b, l, m = x.shape
            r = (m + 1) // 2
            x = jnp.pad(x, ((0, 0), (0, 0), (0, 1))).reshape(b, l * (m + 1))
            x = jnp.pad(x, ((0, 0), (0, m - l))).reshape(b, l + 1, m)
            return x[:, :l, -r:]

        def relative_logits_1d(q, rel_k):
            b, h, w, _ = q.shape
            r = (rel_k.shape[0] + 1) // 2
            logits = jnp.einsum('bxyd,rd->bxyr', q, rel_k)
            logits = rel_to_abs(logits.reshape(b * h, w, 2 * r - 1)).reshape(b, h, w, r)
            return jnp.broadcast_to(logits[:, :, None, :, :], (b, h, r, w, r))

        def rel_pos_emb(q, rel_height, rel_width):
            b = q.shape[0]
            q2 = q.reshape(b, WS, WS, DH)
            lw = relative_logits_1d(q2, rel_width)
            lw = lw.transpose(0, 1, 3, 2, 4).reshape(b, WS * WS, OWS * OWS)
            lh = relative_logits_1d(q2.transpose(0, 2, 1, 3), rel_height)
            lh = lh.transpose(0, 3, 1, 4, 2).reshape(b, WS * WS, OWS * OWS)
            return lw + lh

        def unfold_windows(x):
            b, c, H, W = x.shape
            xp = jnp.pad(x, ((0, 0), (0, 0), (PAD, PAD), (PAD, PAD)))
            nW = (H + 2 * PAD - OWS) // WS + 1
            idx = (jnp.arange(nW) * WS)[:, None] + jnp.arange(OWS)[None, :]
            w = xp[:, :, idx[:, :, None, None], idx[None, None, :, :]]
            w = w.transpose(0, 2, 4, 3, 5, 1)
            return w.reshape(b * nW * nW, OWS * OWS, c)

        def split_heads(t):
            B, n, _ = t.shape
            return t.reshape(B, n, HEADS, DH).transpose(0, 2, 1, 3).reshape(B * HEADS, n, DH)
        b, c, H, W = x.shape
        nW = H // WS
        qkv = jnp.einsum('bchw,oc->bohw', x, W_qkv)
        q, k, v = jnp.split(qkv, 3, axis=1)
        q = q.reshape(b, INNER, nW, WS, nW, WS).transpose(0, 2, 4, 3, 5, 1)
        q = q.reshape(b * nW * nW, WS * WS, INNER)
        k = unfold_windows(k)
        v = unfold_windows(v)
        q, k, v = (split_heads(q), split_heads(k), split_heads(v))
        q = q * SCALE
        attn = jnp.einsum('bnd,bmd->bnm', q, k)
        attn = attn + rel_pos_emb(q, rel_height, rel_width) + FIXED_MASK
        attn = jax.nn.softmax(attn, axis=-1)
        out = jnp.einsum('bnm,bmd->bnd', attn, v)
        out = out.reshape(b, nW, nW, HEADS, WS, WS, DH)
        out = out.transpose(0, 3, 6, 1, 4, 2, 5).reshape(b, INNER, H, W)
        return jnp.einsum('bchw,oc->bohw', out, W_out)

    def _L1_conv_ref(x, weight, bias):
        import jax, jax.numpy as jnp
        import numpy as np
        TILE = 32
        THRESHOLD = 1e-06

        def _tile_mask(x):
            N, C, H, W = x.shape
            xb = jnp.abs(x).reshape(N, C, H // TILE, TILE, W // TILE, TILE)
            active = xb.max(axis=(1, 3, 5)) > THRESHOLD
            m = jnp.repeat(jnp.repeat(active, TILE, axis=1), TILE, axis=2)
            return m[:, None, :, :].astype(x.dtype)
        x_sp = x * _tile_mask(x)
        y = jax.lax.conv_general_dilated(x_sp, weight, window_strides=(1, 1), padding=((1, 1), (1, 1)), dimension_numbers=('NCHW', 'OIHW', 'NCHW'))
        return y + bias[None, :, None, None]

    def _gn(v, G=32, eps=1e-5):
        B_, C_, H_, W_ = v.shape
        g = v.reshape(B_, G, C_ // G, H_, W_)
        m = jnp.mean(g, axis=(2, 3, 4), keepdims=True)
        s = jnp.var(g, axis=(2, 3, 4), keepdims=True)
        return ((g - m) / jnp.sqrt(s + eps)).reshape(v.shape)

    def _ln_c(v, eps=1e-6):
        m = jnp.mean(v, axis=1, keepdims=True)
        s = jnp.var(v, axis=1, keepdims=True)
        return (v - m) / jnp.sqrt(s + eps)

    def _ln_t(v, eps=1e-5):
        m = jnp.mean(v, axis=-1, keepdims=True)
        s = jnp.var(v, axis=-1, keepdims=True)
        return (v - m) / jnp.sqrt(s + eps)

    def _to_tokens(v):
        B_, C_, H_, W_ = v.shape
        return v.reshape(B_, C_, H_ * W_).transpose(0, 2, 1)
    def _from_tokens(t, like):
        B_, C_, H_, W_ = like.shape
        return t.transpose(0, 2, 1).reshape(B_, C_, H_, W_)

    x = x + _L0_conv_ref(_gn(x), L0_conv_W_qkv, L0_conv_W_out, L0_conv_rel_height, L0_conv_rel_width)
    x = x + _L1_conv_ref(_gn(x), L1_conv_weight, L1_conv_bias)
    return x


_drawn_inputs = setup_inputs


def setup_inputs(seed=0):
    import zlib

    import numpy as np

    out = dict(_drawn_inputs(seed))
    spreads = {}
    factors = {'L1_conv_bias': 3.978}
    for name, (base, spread) in spreads.items():
        noise = np.random.default_rng([zlib.crc32(name.encode()), seed]).standard_normal(out[name].shape)
        drawn = base * np.exp(spread * noise) if base else spread * noise
        out[name] = jnp.asarray(drawn.astype(out[name].dtype))
    for name, factor in factors.items():
        out[name] = (out[name] * factor).astype(out[name].dtype)
    return out
```

```python
from contextlib import ExitStack

import concourse.bass as bass
from concourse import mybir

F32 = mybir.dt.float32
F16 = mybir.dt.float16
U32 = mybir.dt.uint32
ALU = mybir.AluOpType
ACT = mybir.ActivationFunctionType
AX = mybir.AxisListType
RMAX = bass.bass_isa.ReduceOp.max

B, C, H, W = 2, 128, 256, 256
HEADS, DH = 4, 32
WS, PAD = 8, 2
GROUP = C // 32
EPS = 1e-5
TILE, THRESHOLD = 32, 1e-6

PAR = 4
QS, KS = WS // 2, (WS + 2 * PAD) // 2
QN, KN = QS * QS, KS * KS
RN = QS + KS - 1
KR = KN + 2 * RN

ROWS = B * H
STRIPS = ROWS // WS
UNITS = 2 * STRIPS
UW = W // 2
NW = UW // WS
GW = 4
GROUPS = NW // GW
LC = UW + PAD
ZR = WS + 2 * PAD
PJ = (UW + 2 * PAD) // 2
PLANE = PJ * KS
QP = QS * UW // 2
KV = KS * (GW * QS + 2)
WK = KS * QS
PAIRS = 2 * GW
DSLOT = KV + WK
QB = C // 2
QBW = QB + 2 * QB * PAR * NW

CROWS = 8
CSTRIPS = ROWS // CROWS
CW = W + 2
TC = W // TILE


def view(t, p0, p1, off, dims):
    base = t[p0:p1, 0:1]
    return bass.AP(base.tensor, base.offset + off, [list(base.ap[0])] + [list(d) for d in dims])


def settled(eng, value):
    return value if isinstance(value, int) else eng.snap(value)


def need(eng, sem, value):
    if isinstance(value, int) and value <= 0:
        return
    eng.wait_ge(sem, value)


def conv_preact_program(nc, x_in, wqkv_in, wout_in, rel_in, wconv_in, bias_in, ident_in, gsum_in,
                        heads_in, shift_in, edge_in, x1_dram, out):
    with ExitStack() as ctx:
        def sb(name, cols, dt, stack=ctx):
            return stack.enter_context(nc.sbuf_tensor(f"sb_{name}", [128, cols], dt))

        wq_h, wq_l = sb("wq_h", 3 * C, F16), sb("wq_l", 3 * C, F16)
        wo_h, wo_l = sb("wo_h", C, F16), sb("wo_l", C, F16)
        wc_h, wc_l = sb("wc_h", 9 * C, F16), sb("wc_l", 9 * C, F16)
        rel_h, rel_l = sb("rel_h", 2 * RN, F16), sb("rel_l", 2 * RN, F16)
        bias = sb("bias", 1, F32)
        ident = sb("ident", 128, F16)
        gsum = sb("gsum", 128, F32)
        heads = sb("heads", HEADS, F16)
        shift = sb("shift", 2 * QS, F32)
        edge = sb("edge", 2 * STRIPS, F32)
        amax = sb("amax", 3, F32)
        amax_all = sb("amax_all", 3, F32)
        wscale = sb("wscale", 3, F32)
        winv = sb("winv", 3, F32)
        alpha = sb("alpha", 1, F32)
        oscale = sb("oscale", 1, F32)
        stats = sb("stats", UNITS * 2 * 6, F32)
        aggr = sb("aggr", 2 * B, F32)
        moments = sb("moments", 2 * B, F32)
        gn = [sb(f"gn{j}", B, F32) for j in range(8)]
        mean_t = sb("mean_t", STRIPS, F32)
        rstd_t = sb("rstd_t", 3 * STRIPS, F32)
        tmax = sb("tmax", UNITS * 4, F32)
        tmin = sb("tmin", UNITS * 4, F32)

        def groupnorm_moments(phase):
            agg_done, sum_done, step_done, sqrt_done = (
                ctx.enter_context(nc.semaphore(f"{phase}_{n}")) for n in ("agg_done", "sum_done", "step_done", "sqrt_done"))
            with nc.psum_tensor(f"{phase}_ps", [128, 512], F32) as ps, nc.Block() as block:
                @block.vector
                def _(dve):
                    k = 0

                    def link(ins):
                        nonlocal k
                        k += 1
                        ins.then_inc(step_done, 1)
                        dve.wait_ge(step_done, k)
                    half = UNITS * 6
                    for b in range(B):
                        link(dve.bn_aggr(aggr[:, 2 * b:2 * b + 2], stats[:, b * half:(b + 1) * half]))
                    mean = view(aggr, 0, 128, 0, [[2, B]])
                    var = view(aggr, 0, 128, 1, [[2, B]])
                    link(dve.tensor_tensor(gn[0][:], mean, mean, ALU.mult))
                    dve.tensor_tensor(var, var, gn[0][:], ALU.add).then_inc(agg_done, 1)
                    dve.wait_ge(sum_done, 1)
                    link(dve.tensor_scalar(moments[:], ps[:, 0:2 * B], 1.0 / GROUP, None, ALU.mult))
                    gmean = view(moments, 0, 128, 0, [[2, B]])
                    gsq = view(moments, 0, 128, 1, [[2, B]])
                    link(dve.tensor_tensor(gn[1][:], gmean, gmean, ALU.mult))
                    link(dve.tensor_tensor(gn[2][:], gsq, gn[1][:], ALU.subtract))
                    link(dve.tensor_scalar(gn[2][:], gn[2][:], 0.0, EPS, ALU.max, ALU.add))
                    link(dve.reciprocal(gn[3][:], gn[2][:]))
                    dve.wait_ge(sqrt_done, 1)
                    for _ in range(2):
                        link(dve.tensor_tensor(gn[4][:], gn[5][:], gn[5][:], ALU.mult))
                        link(dve.tensor_tensor(gn[4][:], gn[4][:], gn[2][:], ALU.mult))
                        link(dve.tensor_scalar(gn[4][:], gn[4][:], -0.5, 1.5, ALU.mult, ALU.add))
                        link(dve.tensor_tensor(gn[5][:], gn[5][:], gn[4][:], ALU.mult))
                    hs = STRIPS // B
                    for b in range(B):
                        link(dve.tensor_copy(mean_t[:, b * hs:(b + 1) * hs],
                                             view(moments, 0, 128, 2 * b, [[0, hs]])))
                        link(dve.tensor_copy(rstd_t[:, STRIPS + b * hs:STRIPS + (b + 1) * hs],
                                             view(gn[5], 0, 128, b, [[0, hs]])))
                    link(dve.tensor_tensor(rstd_t[:, 0:STRIPS], rstd_t[:, STRIPS:2 * STRIPS],
                                           edge[:, 0:STRIPS], ALU.mult))
                    link(dve.tensor_tensor(rstd_t[:, 2 * STRIPS:], rstd_t[:, STRIPS:2 * STRIPS],
                                           edge[:, STRIPS:], ALU.mult))

                @block.tensor
                def _(pe):
                    pe.wait_ge(agg_done, 1)
                    pe.matmul(ps[:, 0:2 * B], gsum[:], aggr[:], start=True, stop=True).then_inc(sum_done, 1)

                @block.scalar
                def _(act):
                    act.wait_ge(step_done, 8)
                    act.activation(gn[5][:], gn[3][:], ACT.Sqrt).then_inc(sqrt_done, 1)

        A_ROWS, A_RING = 16, 4
        A_TILES = ROWS // A_ROWS
        with ExitStack() as pa:
            raw = sb("raw", 3 * C + 2 * RN + C + 9 * C, F32, pa)
            rawn = sb("rawn", 3 * C + 2 * RN + C + 9 * C, F32, pa)
            abuf = sb("abuf", A_RING * A_ROWS * W, F32, pa)
            w_loaded = ctx.enter_context(nc.semaphore("w_loaded"))
            x_loaded = [ctx.enter_context(nc.semaphore(f"a_x_loaded{r}")) for r in range(A_RING)]
            x_used = ctx.enter_context(nc.semaphore("a_x_used"))
            max_done = ctx.enter_context(nc.semaphore("w_max_done"))
            all_done = ctx.enter_context(nc.semaphore("w_all_done"))
            w_step = ctx.enter_context(nc.semaphore("w_step"))
            w_hi = ctx.enter_context(nc.semaphore("w_hi"))
            w_norm = ctx.enter_context(nc.semaphore("w_norm"))
            SPANS = [(0, 3 * C + 2 * RN), (3 * C + 2 * RN, 4 * C + 2 * RN), (4 * C + 2 * RN, 13 * C + 2 * RN)]
            PARTS = [(0, 3 * C, wq_h, wq_l), (3 * C, 3 * C + 2 * RN, rel_h, rel_l),
                     (SPANS[1][0], SPANS[1][1], wo_h, wo_l), (SPANS[2][0], SPANS[2][1], wc_h, wc_l)]
            with nc.Block() as block:
                @block.sync
                def _(sp):
                    sp.dma_start(raw[:, 0:3 * C], wqkv_in).then_inc(w_loaded, 16)
                    sp.dma_start(raw[:, 3 * C:3 * C + 2 * RN], rel_in).then_inc(w_loaded, 16)
                    sp.dma_start(raw[:, SPANS[1][0]:SPANS[1][1]], wout_in).then_inc(w_loaded, 16)
                    sp.dma_start(raw[:, SPANS[2][0]:SPANS[2][1]], wconv_in).then_inc(w_loaded, 16)
                    sp.dma_start(bias[:], bias_in).then_inc(w_loaded, 16)
                    sp.dma_start(ident[:], ident_in).then_inc(w_loaded, 16)
                    sp.dma_start(gsum[:], gsum_in).then_inc(w_loaded, 16)
                    sp.dma_start(heads[:], heads_in).then_inc(w_loaded, 16)
                    sp.dma_start(shift[:], shift_in).then_inc(w_loaded, 16)
                    sp.dma_start(edge[:], edge_in).then_inc(w_loaded, 16)

                    def load(row, r):
                        sp.dma_start(abuf[:, r * A_ROWS * W:(r + 1) * A_ROWS * W],
                                     x_in[:, bass.ds(row, A_ROWS), :]
                                     .rearrange("p a b -> p (a b)")).then_inc(x_loaded[r], 16)
                    for r in range(A_RING):
                        load(r * A_ROWS + PAD, r)
                    with sp.Fori(0, A_TILES // A_RING - 1) as i:
                        for r in range(A_RING):
                            row = sp.snap((i * A_RING + (A_RING + r)) * A_ROWS + PAD)
                            sp.wait_ge(x_used, i * A_RING + r + 1)
                            load(row, r)

                @block.vector
                def _(dve):
                    dve.wait_ge(w_loaded, 10 * 16)
                    for j, (a, b) in enumerate(SPANS):
                        last = dve.tensor_reduce(amax[:, j:j + 1], raw[:, a:b], AX.X, ALU.max,
                                                 apply_absolute_value=True)
                    last.then_inc(max_done, 1)
                    with dve.Fori(0, A_TILES // A_RING) as i:
                        for r in range(A_RING):
                            dve.wait_ge(x_loaded[r], i * 16 + 16)
                            for c in range(A_ROWS * W // 512):
                                last = dve.bn_stats(
                                    stats[:, bass.ds(i * (A_RING * A_ROWS * W // 512 * 6)
                                                     + (r * A_ROWS * W // 512 + c) * 6, 6)],
                                    abuf[:, r * A_ROWS * W + c * 512:r * A_ROWS * W + (c + 1) * 512])
                            last.then_inc(x_used, 1)
                    dve.wait_ge(all_done, 1)
                    dve.tensor_scalar(amax_all[:], amax_all[:], 1e-30, None, ALU.max).then_inc(w_step, 1)
                    dve.wait_ge(w_step, 1)
                    dve.tensor_scalar(wscale[:].bitcast(U32), amax_all[:].bitcast(U32), 0x7F800000, None,
                                      ALU.bitwise_and).then_inc(w_step, 1)
                    dve.wait_ge(w_step, 2)
                    dve.reciprocal(winv[:], wscale[:]).then_inc(w_step, 1)
                    dve.tensor_scalar(alpha[:], wscale[:, 0:1], wscale[:, 0:1], DH ** -0.5, ALU.mult,
                                      ALU.mult).then_inc(w_step, 1)
                    dve.tensor_tensor(oscale[:], wscale[:, 0:1], wscale[:, 1:2], ALU.mult).then_inc(w_step, 1)
                    dve.wait_ge(w_step, 5)
                    for j, (a, b) in enumerate(SPANS):
                        last = dve.tensor_scalar(rawn[:, a:b], raw[:, a:b], winv[:, j:j + 1], None, ALU.mult)
                    last.then_inc(w_norm, 1)
                    dve.wait_ge(w_norm, 1)
                    for a, b, hi, _ in PARTS:
                        dve.tensor_copy(hi[:], rawn[:, a:b]).then_inc(w_hi, 1)
                    dve.wait_ge(w_hi, len(PARTS))
                    for a, b, hi, lo in PARTS:
                        dve.tensor_tensor(lo[:], rawn[:, a:b], hi[:], ALU.subtract)

                @block.gpsimd
                def _(pool):
                    pool.wait_ge(max_done, 1)
                    pool.partition_all_reduce(amax_all[:], amax[:], 128, RMAX).then_inc(all_done, 1)
            groupnorm_moments("gn0")

        with ExitStack() as pb:
            names = ("zf_done", "zh_done", "zl_done", "q_mm", "qh_done", "ql_done",
                     "k_mm", "kh_done", "kl_done", "qbh_done", "qbl_done", "s_mm", "rel_out", "prod_done", "b_done", "e_done",
                     "s2_done", "max_done", "sub_done", "exp_done", "sum_done", "rcp_done", "norm_done",
                     "ph_done", "pl_done", "t_mm", "pt0_done", "pt1_done", "v_mm", "vh_done", "vl_done",
                     "o_mm", "ext_done", "oh_done", "ol_done", "y_mm", "x1_done", "x1_read", "x1_stored",
                     "zeroed")
            sem = {n: pb.enter_context(nc.semaphore(f"b_{n}")) for n in names}
            x_loaded, xr_loaded = ([pb.enter_context(nc.semaphore(f"b_{n}{h}")) for h in range(2)]
                                   for n in ("x_loaded", "xr_loaded"))
            xb = sb("xb", 2 * ZR * LC, F32, pb)
            zf = sb("zf", ZR * LC, F32, pb)
            zh, zl = sb("zh", 4 * PAR * PLANE, F16, pb), sb("zl", 4 * PAR * PLANE, F16, pb)
            qh, ql = sb("qh", PAR * QP, F16, pb), sb("ql", PAR * QP, F16, pb)
            KU = PAR * NW * KR
            kh, kl = sb("kh", 2 * KU, F16, pb), sb("kl", 2 * KU, F16, pb)
            qbh, qbl = sb("qbh", 2 * QBW, F16, pb), sb("qbl", 2 * QBW, F16, pb)
            NS = PAIRS * KN
            rel = sb("rel", 2 * PAIRS * 2 * RN, F32, pb)
            prod = sb("prod", 2 * PAIRS * KS * QS, F32, pb)
            brel = sb("brel", 2 * PAIRS * KS, F32, pb)
            erel = sb("erel", NS, F32, pb)
            sp_ = sb("scores", 2 * NS, F32, pb)
            smax = sb("smax", 2 * PAIRS, F32, pb)
            ssum = sb("ssum", 2 * PAIRS, F32, pb)
            srcp = sb("srcp", 2 * PAIRS, F32, pb)
            DB = PAIRS * DSLOT
            dh, dl = sb("dh", 2 * DB, F16, pb), sb("dl", 2 * DB, F16, pb)
            pt = sb("pt", 2 * 2048, F16, pb)
            vh, vl = sb("vh", 2 * 512, F16, pb), sb("vl", 2 * 512, F16, pb)
            of = sb("of", 2 * 256, F32, pb)
            oh, ol = sb("oh", 2 * 1024, F16, pb), sb("ol", 2 * 1024, F16, pb)
            x1 = sb("x1", 2 * WS * UW, F32, pb)

            def ps(name, cols=512, dt=F32):
                return pb.enter_context(nc.psum_tensor(name, [128, cols], dt))
            ps_q, ps_k, ps_v = ps("ps_q"), ps("ps_k"), ps("ps_v")
            ps_s = [ps("ps_s0"), ps("ps_s1")]
            ps_t = ps("ps_t", 1024, F16)
            ps_o = ps("ps_o", 1024)

            FIRST, LOOP = 6, 4
            TURNS = (UNITS - 3 - FIRST) // LOOP
            GT = UNITS * GROUPS

            def units(eng, body):
                for u in range(-3, FIRST):
                    body(u, u // 2, u % 4, lambda v, top: 0 <= v < top)
                with eng.Fori(0, TURNS) as i:
                    for c in range(LOOP):
                        body(i * LOOP + (FIRST + c), i * (LOOP // 2) + (FIRST + c) // 2, (FIRST + c) % 4,
                             lambda v, top: True)
                for u in range(FIRST + LOOP * TURNS, UNITS + 4):
                    body(u, u // 2, u % 4, lambda v, top: 0 <= v < top)

            def z_plane(t, slot, p, off, dims, p1=128):
                return view(t, 0, p1, (slot % 4) * PAR * PLANE + p * PLANE + off, dims)

            block = pb.enter_context(nc.Block())

            @block.sync
            def _(sp):
                def body(u, s, slot, on):
                    h = slot % 2
                    if on(u + 3, UNITS):
                        row = settled(sp, (s + (h + 3) // 2) * WS)
                        need(sp, sem["zf_done"], u + 2)
                        r = (slot + 3) % 2
                        sp.dma_start(view(xb, 0, 128, r * ZR * LC, [[LC, ZR], [1, LC]]),
                                     x_in[:, bass.ds(row, ZR),
                                          (UW - PAD) * r:(UW - PAD) * r + LC]).then_inc(x_loaded[r], 16)
                    if on(u - 3, UNITS):
                        row = settled(sp, (s - 1 - (1 - h)) * WS + 1)
                        sp.wait_ge(sem["x1_done"], (u - 2) * PAR)
                        sp.dma_start(x1_dram[:, bass.ds(row, WS), UW * (1 - h):UW * (1 - h) + UW],
                                     view(x1, 0, 128, (1 - h) * WS * UW, [[UW, WS], [1, UW]])
                                     ).then_inc(sem["x1_stored"], 16)
                    if on(u - 1, UNITS):
                        row = settled(sp, (s + (h - 1) // 2) * WS + PAD)
                        done = settled(sp, (u - 2) * 16)
                        need(sp, sem["x1_read"], done)
                        need(sp, sem["x1_stored"], done)
                        r = (slot + 3) % 2
                        sp.dma_start(view(x1, 0, 128, r * WS * UW, [[UW, WS], [1, UW]]),
                                     x_in[:, bass.ds(row, WS),
                                          UW * r:UW * r + UW]).then_inc(xr_loaded[r], 16)
                units(sp, body)
                sp.wait_ge(sem["x1_stored"], UNITS * 16)

            @block.tensor
            def _(pe):
                def project(p, slot, u, side):
                    piece = u * PAR + p
                    if p == 0:
                        pe.wait_ge(sem["zl_done"], u + 1)
                    need(pe, sem["ql_done"], piece)
                    if p in Y_BEFORE:
                        need(pe, sem["x1_done"], Y_BEFORE[p] + (u - 3) * PAR)
                    dq = [[KS, UW // 2], [1, QS]]
                    q_at = lambda z: z_plane(z, slot, p, KS + 1, dq)
                    pe.matmul(ps_q[:, 0:QP], wq_h[:, 0:C], q_at(zh), start=True, stop=False)
                    pe.matmul(ps_q[:, 0:QP], wq_h[:, 0:C], q_at(zl), start=False, stop=False)
                    pe.matmul(ps_q[:, 0:QP], wq_l[:, 0:C], q_at(zh), start=False, stop=True).then_inc(sem["q_mm"], 1)
                    need(pe, sem["kl_done"], piece)
                    k_at = lambda z: z_plane(z, slot, p, 0, [[1, PLANE]])
                    pe.matmul(ps_k[:, 0:PLANE], wq_h[:, C:2 * C], k_at(zh), start=True, stop=False)
                    pe.matmul(ps_k[:, 0:PLANE], wq_h[:, C:2 * C], k_at(zl), start=False, stop=False)
                    pe.matmul(ps_k[:, 0:PLANE], wq_l[:, C:2 * C], k_at(zh), start=False,
                              stop=True).then_inc(sem["k_mm"], 1)

                def transposes(m, par, py):
                    if py == 0:
                        pe.wait_ge(sem["pl_done"], m + 1)
                        need(pe, sem["pt1_done"], m)
                    else:
                        pe.wait_ge(sem["pt0_done"], m + 1)
                    for wj in range(GW):
                        pr = py * GW + wj
                        at = pr * DSLOT - WK * wj
                        for part, d in enumerate((dh, dl)):
                            last = pe.transpose(ps_t[0:KV, (2 * wj + part) * 128:(2 * wj + part + 1) * 128],
                                                d[:, par * DB + at:par * DB + at + KV], ident[:])
                    last.then_inc(sem["t_mm"], 1)

                def body(u, s, slot, on):
                    for g in range(GROUPS):
                        n = u * GROUPS + g
                        if on(n, GT):
                            if g == 0:
                                pe.wait_ge(sem["qbh_done"], u + 1)
                                pe.wait_ge(sem["qbl_done"], u + 1)
                                pe.wait_ge(sem["kl_done"], (u + 1) * PAR)
                            need(pe, sem["s2_done"], n - 1)
                            ub = slot % 2
                            for pr in range(PAIRS):
                                py, wj = divmod(pr, GW)
                                s_at = ps_s[g % 2][:, pr * KR:(pr + 1) * KR]
                                for px in range(2):
                                    p, w = 2 * py + px, GW * g + wj
                                    qc = ub * QBW + (p * NW + w) * 2 * QB + (QB if px == 0 else 0)
                                    kc = ub * KU + (p * NW + w) * KR
                                    terms = ((qbh, kh), (qbh, kl), (qbl, kh))
                                    for t, (q, k) in enumerate(terms):
                                        last = pe.matmul(s_at, q[:, qc:qc + 2 * QB], k[:, kc:kc + KR],
                                                         start=(px == 0 and t == 0), stop=(px == 1 and t == 2))
                            last.then_inc(sem["s_mm"], 1)
                        if on(n - 3, GT):
                            transposes(n - 3, (g - 3) % 2, 0)
                        if g < 2 and on(u + 1, UNITS):
                            project(2 * g, slot + 1, u + 1, (slot + 1) % 2)
                        if on(n - 3, GT):
                            m = n - 3
                            vslot, vg = (slot, 0) if g == 3 else (slot - 1, g + 1)
                            need(pe, sem["vl_done"], m)
                            for p in range(PAR):
                                z_at = lambda z: z_plane(z, vslot, p, GW * WK * vg, [[1, KV]])
                                v_out = ps_v[0:KV, p * C:(p + 1) * C]
                                pe.matmul(v_out, z_at(zh), wq_h[:, 2 * C:3 * C], start=True, stop=False)
                                pe.matmul(v_out, z_at(zh), wq_l[:, 2 * C:3 * C], start=False, stop=False)
                                last = pe.matmul(v_out, z_at(zl), wq_h[:, 2 * C:3 * C], start=False, stop=True)
                            last.then_inc(sem["v_mm"], 1)
                        if on(n - 4, GT):
                            m, par = n - 4, g % 2
                            pe.wait_ge(sem["pt1_done"], m + 1)
                            pe.wait_ge(sem["vl_done"], m + 1)
                            need(pe, sem["ext_done"], m)
                            for p in range(PAR):
                                py, px = divmod(p, 2)
                                o_at = ps_o[:, p * 256:(p + 1) * 256]
                                v_at = lambda v: v[0:KV, par * 512 + p * C:par * 512 + (p + 1) * C]
                                p_at = lambda part: view(pt, 0, KV, par * 2048 + py * 1024 + part * 128 + px * 64,
                                                         [[256, GW], [1, QB]])
                                pe.matmul(o_at, v_at(vh), p_at(0), start=True, stop=False)
                                pe.matmul(o_at, v_at(vh), p_at(1), start=False, stop=False)
                                last = pe.matmul(o_at, v_at(vl), p_at(0), start=False, stop=True)
                            last.then_inc(sem["o_mm"], 1)
                        if on(n - 3, GT):
                            transposes(n - 3, (g - 3) % 2, 1)
                        if g < 2 and on(u + 1, UNITS):
                            project(2 * g + 1, slot + 1, u + 1, (slot + 1) % 2)
                        if on(u - 2, UNITS):
                            piece = (u - 2) * PAR + g
                            if g == 0:
                                pe.wait_ge(sem["ol_done"], (u - 1) * GROUPS)
                            if g < 2:
                                need(pe, sem["ql_done"], QL_BEFORE(u, g))
                            need(pe, sem["x1_done"], piece)
                            ob = slot % 2
                            o_rhs = lambda o: o[:, ob * 1024 + g * QP:ob * 1024 + (g + 1) * QP]
                            pe.matmul(ps_q[:, 0:QP], wo_h[:], o_rhs(oh), start=True, stop=False)
                            pe.matmul(ps_q[:, 0:QP], wo_h[:], o_rhs(ol), start=False, stop=False)
                            pe.matmul(ps_q[:, 0:QP], wo_l[:], o_rhs(oh), start=False, stop=True
                                      ).then_inc(sem["y_mm"], 1)
                Y_BEFORE = {0: 0, 2: 1}

                def QL_BEFORE(u, g):
                    if not isinstance(u, int):
                        return (u + 1) * PAR + 2 * g + 2
                    return min((u + 1) * PAR + 2 * g + 2, UNITS * PAR)
                pe.wait_ge(sem["zeroed"], 3)
                units(pe, body)

            @block.vector
            def _(dve):
                for t in (zh, zl):
                    for slot in range(4):
                        last = dve.memset(view(t, 0, 128, slot * PAR * PLANE + (slot % 2) * (PJ - 1) * KS,
                                               [[PLANE, PAR], [1, KS]]), 0.0)
                for t in (dh, dl):
                    last = dve.memset(t[:], 0.0)
                for t, src in ((kh, rel_h), (kl, rel_l)):
                    for b in range(2):
                        last = dve.tensor_copy(view(t, 0, 128, b * KU + KN, [[KR, PAR * NW], [1, 2 * RN]]),
                                               view(src, 0, 128, 0, [[0, PAR * NW], [1, 2 * RN]]))
                last.then_inc(sem["zeroed"], 1)

                def low_parts(u, h, p):
                    piece = (u + 1) * PAR + p
                    if p == 0:
                        need(dve, sem["qbl_done"], u + 1)
                    dve.wait_ge(sem["qh_done"], piece + 1)
                    dve.tensor_tensor(ql[:, p * QP:(p + 1) * QP], ps_q[:, 0:QP],
                                      qh[:, p * QP:(p + 1) * QP], ALU.subtract).then_inc(sem["ql_done"], 1)
                    dve.wait_ge(sem["kh_done"], piece + 1)
                    k_off = (1 - h) * KU + p * NW * KR
                    k_dims = [[KR, NW], [1, KN]]
                    dve.tensor_tensor(view(kl, 0, 128, k_off, k_dims),
                                      view(ps_k, 0, 128, 0, [[WK, NW], [1, KN]]),
                                      view(kh, 0, 128, k_off, k_dims), ALU.subtract).then_inc(sem["kl_done"], 1)

                def body(u, s, slot, on):
                    h = slot % 2
                    for g in range(GROUPS):
                        n = u * GROUPS + g
                        b0 = g % 2
                        b1 = 1 - b0
                        nn = slice(b0 * NS, (b0 + 1) * NS)
                        n8 = slice(b0 * PAIRS, (b0 + 1) * PAIRS)
                        spread = lambda t: view(t, 0, 128, b0 * PAIRS, [[1, PAIRS], [0, KN]])
                        by_pair = lambda t, b: view(t, 0, 128, b * NS, [[KN, PAIRS], [1, KN]])
                        if on(u - 2 if g else u - 3, UNITS):
                            xu, xp, xh = (u - 2, g - 1, h) if g else (u - 3, PAR - 1, 1 - h)
                            if xp == 0:
                                dve.wait_ge(xr_loaded[h], s * 16)
                            dve.wait_ge(sem["y_mm"], xu * PAR + xp + 1)
                            off = xh * WS * UW + (xp // 2) * UW + xp % 2
                            dims = [[2 * UW, QS], [2, UW // 2]]
                            dve.scalar_tensor_tensor(view(x1, 0, 128, off, dims),
                                                     view(ps_q, 0, 128, 0, [[1, QS], [QS, UW // 2]]),
                                                     oscale[:, 0:1], view(x1, 0, 128, off, dims), ALU.mult, ALU.add
                                                     ).then_inc(sem["x1_done"], 1)
                        if on(n - 1, GT):
                            dve.wait_ge(sem["prod_done"], n)
                            dve.tensor_reduce(brel[:], view(prod, 0, 128, 0, [[QS, 2 * PAIRS * KS], [1, QS]]),
                                              AX.X, ALU.add).then_inc(sem["b_done"], 1)
                        if on(n - 2, GT):
                            dve.wait_ge(sem["exp_done"], n - 1)
                            dve.tensor_reduce(ssum[:, n8], by_pair(sp_, b0), AX.X, ALU.add
                                              ).then_inc(sem["sum_done"], 1)
                        if on(n, GT):
                            dve.wait_ge(sem["s_mm"], n + 1)
                            need(dve, sem["prod_done"], n - 1)
                            dve.tensor_copy(view(rel, 0, 128, b0 * PAIRS * 2 * RN, [[2 * RN, PAIRS], [1, 2 * RN]]),
                                            view(ps_s[g % 2], 0, 128, KN, [[KR, PAIRS], [1, 2 * RN]])
                                            ).then_inc(sem["rel_out"], 1)
                        if on(n - 2, GT):
                            dve.wait_ge(sem["sum_done"], n - 1)
                            dve.reciprocal(srcp[:, n8], ssum[:, n8]).then_inc(sem["rcp_done"], 1)
                        if on(n - 2, GT):
                            dve.wait_ge(sem["rcp_done"], n - 1)
                            dve.tensor_tensor(by_pair(sp_, b0), by_pair(sp_, b0), spread(srcp), ALU.mult
                                              ).then_inc(sem["norm_done"], 1)
                        if on(n - 1, GT):
                            dve.wait_ge(sem["e_done"], n)
                            need(dve, sem["pl_done"], n - 2)
                            dve.tensor_tensor(by_pair(sp_, b1), view(ps_s[1 - g % 2], 0, 128, 0, [[KR, PAIRS], [1, KN]]),
                                              view(erel, 0, 128, 0, [[KN, PAIRS], [1, KN]]), ALU.add
                                              ).then_inc(sem["s2_done"], 1)
                        if on(n - 1, GT):
                            dve.wait_ge(sem["s2_done"], n)
                            need(dve, sem["sub_done"], n - 2)
                            dve.tensor_reduce(smax[:, b1 * PAIRS:(b1 + 1) * PAIRS], by_pair(sp_, b1), AX.X, ALU.max
                                              ).then_inc(sem["max_done"], 1)
                        if g == 2 and on(u - 3, UNITS):
                            dve.wait_ge(sem["x1_done"], (u - 2) * PAR)
                            for c in range(2):
                                dve.bn_stats(stats[:, bass.ds((u - 3) * 12 + c * 6, 6)],
                                             x1[:, (1 - h) * WS * UW + c * 512:(1 - h) * WS * UW + (c + 1) * 512])
                        if g >= 2 and on(u - 3, UNITS):
                            t, op = (tmax, ALU.max) if g == 2 else (tmin, ALU.min)
                            last = dve.tensor_reduce(t[:, bass.ds((u - 3) * 4, 4)],
                                              view(x1, 0, 128, (1 - h) * WS * UW, [[TILE, 4], [UW, WS], [1, TILE]]),
                                              AX.XY, op)
                            if g == 3:
                                last.then_inc(sem["x1_read"], 16)
                        if g < 2 and on(u + 1, UNITS):
                            low_parts(u, h, 2 * g)
                        if on(n - 2, GT):
                            dve.wait_ge(sem["ph_done"], n - 1)
                            d_dims = [[DSLOT, PAIRS], [1, KN]]
                            dve.tensor_tensor(view(dl, 0, 128, b0 * DB, d_dims),
                                              view(sp_, 0, 128, b0 * NS, [[KN, PAIRS], [1, KN]]),
                                              view(dh, 0, 128, b0 * DB, d_dims), ALU.subtract
                                              ).then_inc(sem["pl_done"], 1)
                        if on(n - 3, GT):
                            dve.wait_ge(sem["vh_done"], n - 2)
                            dve.tensor_tensor(vl[0:KV, b1 * 512:(b1 + 1) * 512], ps_v[0:KV, :],
                                              vh[0:KV, b1 * 512:(b1 + 1) * 512], ALU.subtract
                                              ).then_inc(sem["vl_done"], 1)
                        if g < 2 and on(u + 1, UNITS):
                            low_parts(u, h, 2 * g + 1)
                        if on(n - 3, GT):
                            dve.wait_ge(sem["t_mm"], 2 * (n - 2))
                            dve.tensor_copy(pt[0:KV, b1 * 2048 + 1024:b1 * 2048 + 2048], ps_t[0:KV, :]
                                            ).then_inc(sem["pt1_done"], 1)
                        if g == 1 and on(u + 2, UNITS):
                            dve.wait_ge(x_loaded[h], (s + 2) * 16)
                            need(dve, sem["zl_done"], u + 2)
                            s2_ = s + 1
                            for part, (r0, r1) in enumerate(((0, PAD), (PAD, ZR - PAD), (ZR - PAD, ZR))):
                                last = dve.tensor_scalar(zf[:, r0 * LC:r1 * LC],
                                                         xb[:, (h * ZR + r0) * LC:(h * ZR + r1) * LC],
                                                         mean_t[:, bass.ds(s2_, 1)],
                                                         rstd_t[:, bass.ds(s2_ + part * STRIPS, 1)],
                                                         ALU.subtract, ALU.mult)
                            last.then_inc(sem["zf_done"], 1)
                dve.wait_ge(sem["zeroed"], 3)
                units(dve, body)

            @block.scalar
            def _(act):
                def high_parts(u, h, p):
                    piece = (u + 1) * PAR + p
                    if p == 0:
                        need(act, sem["qbh_done"], u + 1)
                    act.wait_ge(sem["q_mm"], piece + 1)
                    act.copy(qh[:, p * QP:(p + 1) * QP], ps_q[:, 0:QP]).then_inc(sem["qh_done"], 1)
                    if p == 0:
                        need(act, sem["s_mm"], u * GROUPS)
                    act.wait_ge(sem["k_mm"], piece + 1)
                    act.copy(view(kh, 0, 128, (1 - h) * KU + p * NW * KR, [[KR, NW], [1, KN]]),
                             view(ps_k, 0, 128, 0, [[WK, NW], [1, KN]])).then_inc(sem["kh_done"], 1)

                def body(u, s, slot, on):
                    h = slot % 2
                    for g in range(GROUPS):
                        n = u * GROUPS + g
                        b0, b1 = g % 2, 1 - g % 2
                        if on(n - 2, GT):
                            act.wait_ge(sem["sub_done"], n - 1)
                            act.activation(sp_[:, b0 * NS:(b0 + 1) * NS], sp_[:, b0 * NS:(b0 + 1) * NS], ACT.Exp,
                                           scale=alpha[:, 0:1]).then_inc(sem["exp_done"], 1)
                        if on(n - 3, GT):
                            act.wait_ge(sem["t_mm"], 2 * (n - 3) + 1)
                            need(act, sem["o_mm"], n - 4)
                            act.copy(pt[0:KV, b1 * 2048:b1 * 2048 + 1024], ps_t[0:KV, :]
                                     ).then_inc(sem["pt0_done"], 1)
                        if g == 2 and on(u + 2, UNITS):
                            act.wait_ge(sem["zf_done"], u + 3)
                            need(act, sem["v_mm"], (u - 1) * GROUPS)
                            for py in range(2):
                                off = ((slot + 2) % 4) * PAR * PLANE + 2 * py * PLANE + (1 - h) * KS
                                last = act.copy(view(zh, 0, 128, off, [[PLANE, 2], [KS, LC // 2], [1, KS]]),
                                                view(zf, 0, 128, py * LC, [[1, 2], [2, LC // 2], [2 * LC, KS]]))
                            last.then_inc(sem["zh_done"], 1)
                        if g in (1, 3) and on(u + 1, UNITS):
                            p = 0 if g == 1 else 2
                            if g == 1:
                                need(act, sem["s_mm"], u * GROUPS)
                            act.wait_ge(sem["qh_done"], (u + 1) * PAR + p + 2)
                            for hd in range(HEADS):
                                last = act.copy(view(qbh, DH * hd, DH * hd + DH,
                                                     (1 - h) * QBW + p * NW * 2 * QB + QB + hd * QN,
                                                     [[2 * QB, 2 * NW], [1, QN]]),
                                                view(qh, DH * hd, DH * hd + DH, p * QP, [[QN, 2 * NW], [1, QN]]))
                            if g == 3:
                                last.then_inc(sem["qbh_done"], 1)
                        if on(n - 2, GT):
                            act.wait_ge(sem["norm_done"], n - 1)
                            need(act, sem["t_mm"], 2 * (n - 3))
                            act.copy(view(dh, 0, 128, b0 * DB, [[DSLOT, PAIRS], [1, KN]]),
                                     view(sp_, 0, 128, b0 * NS, [[KN, PAIRS], [1, KN]])
                                     ).then_inc(sem["ph_done"], 1)
                        if g < 2 and on(u + 1, UNITS):
                            high_parts(u, h, 2 * g)
                        if on(n - 3, GT):
                            act.wait_ge(sem["v_mm"], n - 2)
                            need(act, sem["o_mm"], n - 4)
                            act.copy(vh[0:KV, b1 * 512:(b1 + 1) * 512], ps_v[0:KV, :]).then_inc(sem["vh_done"], 1)
                        if on(n - 4, GT):
                            act.wait_ge(sem["o_mm"], n - 3)
                            need(act, sem["ol_done"], n - 5)
                            for hd in range(HEADS):
                                last = act.copy(view(of, DH * hd, DH * hd + DH, b0 * 256, [[QN, PAR * GW], [1, QN]]),
                                                view(ps_o, DH * hd, DH * hd + DH, hd * QN, [[QB, PAR * GW], [1, QN]]))
                            last.then_inc(sem["ext_done"], 1)
                        if g < 2 and on(u + 1, UNITS):
                            high_parts(u, h, 2 * g + 1)
                        if on(n - 4, GT):
                            act.wait_ge(sem["ext_done"], n - 3)
                            need(act, sem["y_mm"], (u - 2) * PAR)
                            act.copy(view(oh, 0, 128, ((slot - 1) % 2) * 1024 + g * GW * QN,
                                          [[QP, PAR], [1, GW * QN]]),
                                     view(of, 0, 128, b0 * 256, [[GW * QN, PAR], [1, GW * QN]])
                                     ).then_inc(sem["oh_done"], 1)
                act.wait_ge(sem["zeroed"], 3)
                units(act, body)

            @block.gpsimd
            def _(pool):
                for t in (qbh, qbl):
                    pool.memset(t[:], 0.0).then_inc(sem["zeroed"], 1)
                pool.wait_ge(sem["zeroed"], 3)

                def layout(u, h, p):
                    if p == 0:
                        need(pool, sem["s_mm"], u * GROUPS)
                    pool.wait_ge(sem["ql_done"], (u + 1) * PAR + p + 1)
                    last = pool.tensor_tensor(
                        view(qbl, 0, 128, (1 - h) * QBW + p * NW * 2 * QB + QB, [[2 * QB, NW], [QN, HEADS], [1, QN]]),
                        view(ql, 0, 128, p * QP, [[QN, NW], [0, HEADS], [1, QN]]),
                        view(heads, 0, 128, 0, [[0, NW], [1, HEADS], [0, QN]]), ALU.mult)
                    if p == PAR - 1:
                        last.then_inc(sem["qbl_done"], 1)

                def body(u, s, slot, on):
                    h = slot % 2
                    for g in range(GROUPS):
                        n = u * GROUPS + g
                        b0, b1 = g % 2, 1 - g % 2
                        if on(n - 1, GT):
                            pool.wait_ge(sem["b_done"], n)
                            need(pool, sem["s2_done"], n - 1)
                            pool.tensor_tensor(view(erel, 0, 128, 0, [[KN, PAIRS], [KS, KS], [1, KS]]),
                                               view(brel, 0, 128, 0, [[KS, PAIRS], [0, KS], [1, KS]]),
                                               view(brel, 0, 128, PAIRS * KS, [[KS, PAIRS], [1, KS], [0, KS]]),
                                               ALU.add).then_inc(sem["e_done"], 1)
                        if on(n, GT):
                            pool.wait_ge(sem["rel_out"], n + 1)
                            need(pool, sem["b_done"], n)
                            for ax in range(2):
                                last = pool.tensor_tensor(
                                    view(prod, 0, 128, ax * PAIRS * KS * QS, [[KS * QS, PAIRS], [QS, KS], [1, QS]]),
                                    view(rel, 0, 128, b0 * PAIRS * 2 * RN + ax * RN, [[2 * RN, PAIRS], [1, KS], [1, QS]]),
                                    view(shift, 0, 128, ax * QS, [[0, PAIRS], [0, KS], [1, QS]]), ALU.mult)
                            last.then_inc(sem["prod_done"], 1)
                        if g in (1, 2) and on(u + 1, UNITS):
                            layout(u, h, 2 * g - 2)
                        if on(n - 1, GT):
                            pool.wait_ge(sem["max_done"], n)
                            pool.tensor_tensor(view(sp_, 0, 128, b1 * NS, [[KN, PAIRS], [1, KN]]),
                                               view(sp_, 0, 128, b1 * NS, [[KN, PAIRS], [1, KN]]),
                                               view(smax, 0, 128, b1 * PAIRS, [[1, PAIRS], [0, KN]]),
                                               ALU.subtract).then_inc(sem["sub_done"], 1)
                        if on(n - 5, GT):
                            pool.wait_ge(sem["oh_done"], n - 4)
                            ob = (slot - (1 if g else 2)) % 2
                            og = (g - 5) % 4
                            o_dims, o_off = [[QP, PAR], [1, GW * QN]], ob * 1024 + og * GW * QN
                            pool.tensor_tensor(view(ol, 0, 128, o_off, o_dims),
                                               view(of, 0, 128, b1 * 256, [[GW * QN, PAR], [1, GW * QN]]),
                                               view(oh, 0, 128, o_off, o_dims), ALU.subtract
                                               ).then_inc(sem["ol_done"], 1)
                        if g in (1, 2) and on(u + 1, UNITS):
                            layout(u, h, 2 * g - 1)
                        if g == 3 and on(u + 2, UNITS):
                            pool.wait_ge(sem["zh_done"], u + 3)
                            for py in range(2):
                                dims = [[PLANE, 2], [KS, LC // 2], [1, KS]]
                                off = ((slot + 2) % 4) * PAR * PLANE + 2 * py * PLANE + (1 - h) * KS
                                last = pool.tensor_tensor(view(zl, 0, 128, off, dims),
                                                          view(zf, 0, 128, py * LC, [[1, 2], [2, LC // 2], [2 * LC, KS]]),
                                                          view(zh, 0, 128, off, dims), ALU.subtract)
                            last.then_inc(sem["zl_done"], 1)
                units(pool, body)
        groupnorm_moments("gn1")

        ctab = sb("ctab", 3 * CSTRIPS * TC, F32)
        TR = ROWS // TILE
        SPT = TILE // CROWS
        with ExitStack() as pf:
            ext = [sb(f"tile_ext{j}", TR * TC, F32, pf) for j in range(2)]
            tabs = sb("tile_abs", TR * TC, F32, pf)
            f_step = ctx.enter_context(nc.semaphore("f_step"))
            f_all = ctx.enter_context(nc.semaphore("f_all"))
            with nc.Block() as block:
                @block.vector
                def _(dve):
                    k = 0

                    def link(ins):
                        nonlocal k
                        k += 1
                        ins.then_inc(f_step, 1)
                        dve.wait_ge(f_step, k)
                    hs = STRIPS // B
                    for t, dst, op in ((tmax, ext[0], ALU.max), (tmin, ext[1], ALU.min)):
                        for h in range(2):
                            link(dve.tensor_reduce(view(dst, 0, 128, 4 * h, [[TC, TR], [1, 4]]),
                                                   view(t, 0, 128, 4 * h, [[2 * SPT * 4, TR], [1, 4], [8, SPT]]),
                                                   AX.X, op))
                        for b in range(B):
                            part = dst[:, b * TR // B * TC:(b + 1) * TR // B * TC]
                            link(dve.tensor_scalar(part, part, mean_t[:, b * hs:b * hs + 1],
                                                   rstd_t[:, STRIPS + b * hs:STRIPS + b * hs + 1],
                                                   ALU.subtract, ALU.mult))
                    link(dve.scalar_tensor_tensor(ext[0][:], ext[1][:], -1.0, ext[0][:], ALU.mult, ALU.max))
                    dve.wait_ge(f_all, 1)
                    link(dve.tensor_scalar(tabs[:], tabs[:], THRESHOLD, None, ALU.is_gt))
                    S8 = CSTRIPS * TC
                    for q in range(SPT):
                        for b in range(B):
                            n = TR // B
                            link(dve.tensor_scalar(view(ctab, 0, 128, S8 + (b * n * SPT + q) * TC, [[SPT * TC, n], [1, TC]]),
                                                   view(tabs, 0, 128, b * n * TC, [[TC, n], [1, TC]]),
                                                   rstd_t[:, STRIPS + b * hs:STRIPS + b * hs + 1], None, ALU.mult))
                    link(dve.tensor_copy(ctab[:, TC:S8], ctab[:, S8:2 * S8 - TC]))
                    link(dve.tensor_copy(ctab[:, 2 * S8:3 * S8 - TC], ctab[:, S8 + TC:2 * S8]))
                    for b in range(B):
                        link(dve.memset(ctab[:, b * S8 // B:b * S8 // B + TC], 0.0))
                        link(dve.memset(ctab[:, 2 * S8 + (b + 1) * S8 // B - TC:2 * S8 + (b + 1) * S8 // B], 0.0))

                @block.gpsimd
                def _(pool):
                    pool.wait_ge(f_step, 9)
                    pool.partition_all_reduce(tabs[:], ext[0][:], 128, RMAX).then_inc(f_all, 1)

        with ExitStack() as pc:
            names = ("zf_done", "zh_done", "zl_done", "conv_mm", "ev_done", "out_done", "pads", "edges")
            sem = {n: pc.enter_context(nc.semaphore(f"c_{n}")) for n in names}
            CZ = CROWS + 2
            BLK = CROWS * W // 512
            XR = 4
            x_loaded = [pc.enter_context(nc.semaphore(f"c_x_loaded{r}")) for r in range(XR)]
            stored = [pc.enter_context(nc.semaphore(f"c_stored{r}")) for r in range(2)]
            xc = sb("xc", XR * CZ * W, F32, pc)
            cf = sb("cf", CZ * W, F32, pc)
            ch, cl = sb("ch", 2 * CZ * CW, F16, pc), sb("cl", 2 * CZ * CW, F16, pc)
            ev = sb("ev", 4 * 512, F32, pc)
            oc = sb("oc", 2 * CROWS * W, F32, pc)
            zrow = sb("zrow", W, F32, pc)
            ps_c = pc.enter_context(nc.psum_tensor("ps_c", [128, 2 * BLK * 512], F32))
            CFIRST, CTURNS = 5, 14

            def strips(eng, body):
                for j in range(-3, CFIRST):
                    body(j, j // XR, j % XR, lambda v: 0 <= v < CSTRIPS)
                with eng.Fori(0, CTURNS) as i:
                    for c in range(XR):
                        body(i * XR + (CFIRST + c), i + (CFIRST + c) // XR, (CFIRST + c) % XR, lambda v: True)
                for j in range(CFIRST + XR * CTURNS, CSTRIPS + 1):
                    body(j, j // XR, j % XR, lambda v: 0 <= v < CSTRIPS)

            block = pc.enter_context(nc.Block())

            @block.sync
            def _(sp):
                sp.wait_ge(sem["pads"], 1)
                sp.dma_start(x1_dram[:, 0:1, :].rearrange("p a b -> p (a b)"), zrow[:]).then_inc(sem["edges"], 16)
                sp.dma_start(x1_dram[:, ROWS + 1:ROWS + 2, :].rearrange("p a b -> p (a b)"), zrow[:]
                             ).then_inc(sem["edges"], 16)
                sp.wait_ge(sem["edges"], 32)

                def body(j, t, slot, on):
                    if on(j + 3):
                        row = settled(sp, (j + 3) * CROWS)
                        need(sp, sem["out_done"], j * BLK)
                        r = (slot + 3) % XR
                        sp.dma_start(xc[:, r * CZ * W:(r + 1) * CZ * W],
                                     x1_dram[:, bass.ds(row, CZ), :].rearrange("p a b -> p (a b)")
                                     ).then_inc(x_loaded[r], 16)
                    if on(j - 1):
                        row = settled(sp, (j - 1) * CROWS)
                        sp.wait_ge(sem["out_done"], j * BLK)
                        o = (slot - 1) % 2
                        sp.dma_start(out[:, bass.ds(row, CROWS), :].rearrange("p a b -> p (a b)"),
                                     oc[:, o * CROWS * W:(o + 1) * CROWS * W]).then_inc(stored[o], 16)
                strips(sp, body)
                for done in stored:
                    sp.wait_ge(done, CSTRIPS // 2 * 16)

            @block.tensor
            def _(pe):
                def body(j, t, slot, on):
                    if not on(j):
                        return
                    pe.wait_ge(sem["zl_done"], j + 1)
                    z0 = (slot % 2) * CZ * CW
                    for q in range(BLK):
                        bank = (slot % 2) * BLK + q
                        need(pe, sem["ev_done"], (j - 2) * BLK + q + 1)
                        o_at = ps_c[:, bank * 512:(bank + 1) * 512]
                        k = 0
                        for tap in range(9):
                            ky, kx = divmod(tap, 3)
                            z_at = lambda z: view(z, 0, 128, z0 + (2 * q + ky) * CW + kx, [[CW, 2], [1, W]])
                            for wt, z in ((wc_h, ch), (wc_h, cl), (wc_l, ch)):
                                last = pe.matmul(o_at, wt[:, tap * C:(tap + 1) * C], z_at(z), start=(k == 0),
                                                 stop=(k == 26))
                                k += 1
                        last.then_inc(sem["conv_mm"], 1)
                strips(pe, body)

            @block.scalar
            def _(act):
                def body(j, t, slot, on):
                    if on(j + 1):
                        act.wait_ge(sem["zf_done"], j + 2)
                        need(act, sem["conv_mm"], j * BLK)
                        o = ((slot + 1) % 2) * CZ * CW
                        act.copy(view(ch, 0, 128, o + 1, [[CW, CZ], [1, W]]),
                                 view(cf, 0, 128, 0, [[W, CZ], [1, W]])).then_inc(sem["zh_done"], 1)
                    if on(j):
                        for q in range(BLK):
                            bank = (slot % 2) * BLK + q
                            act.wait_ge(sem["conv_mm"], j * BLK + q + 1)
                            need(act, sem["out_done"], (j - 1) * BLK + q + 1)
                            act.activation(ev[:, q * 512:(q + 1) * 512], ps_c[:, bank * 512:(bank + 1) * 512],
                                           ACT.Identity, bias=bias[:, 0:1], scale=wscale[:, 2:3]
                                           ).then_inc(sem["ev_done"], 1)
                strips(act, body)

            @block.vector
            def _(dve):
                dve.memset(zrow[:], 0.0)
                for z in (ch, cl):
                    last = dve.memset(view(z, 0, 128, 0, [[CW, 2 * CZ], [CW - 1, 2]]), 0.0)
                last.then_inc(sem["pads"], 1)

                def body(j, t, slot, on):
                    if on(j + 1):
                        dve.wait_ge(x_loaded[(slot + 1) % XR], (t + (slot + 1) // XR + 1) * 16)
                        need(dve, sem["zl_done"], j + 1)
                        r = ((slot + 1) % XR) * CZ * W
                        for part, (r0, rn) in enumerate(((0, 1), (1, CROWS), (CZ - 1, 1))):
                            for tc in range(TC):
                                dims, off = [[W, rn], [1, TILE]], r0 * W + tc * TILE
                                last = dve.tensor_scalar(view(cf, 0, 128, off, dims), view(xc, 0, 128, r + off, dims),
                                                         mean_t[:, bass.ds(j + 1, 1)],
                                                         ctab[:, bass.ds((j + 1) * TC + part * CSTRIPS * TC + tc, 1)],
                                                         ALU.subtract, ALU.mult)
                        last.then_inc(sem["zf_done"], 1)
                    if on(j):
                        for q in range(BLK):
                            if q == 0:
                                need(dve, stored[slot % 2], (t * 2 + slot // 2) * 16)
                            dve.wait_ge(sem["ev_done"], j * BLK + q + 1)
                            o, r = (slot % 2) * CROWS * W, (slot % XR) * CZ * W
                            dve.tensor_tensor(oc[:, o + q * 512:o + (q + 1) * 512], ev[:, q * 512:(q + 1) * 512],
                                              xc[:, r + W + q * 512:r + W + (q + 1) * 512], ALU.add
                                              ).then_inc(sem["out_done"], 1)
                            if q == 0 and on(j + 1):
                                dve.wait_ge(sem["zh_done"], j + 2)
                                zo = ((slot + 1) % 2) * CZ * CW + 1
                                dve.tensor_tensor(view(cl, 0, 128, zo, [[CW, CZ], [1, W]]),
                                                  view(cf, 0, 128, 0, [[W, CZ], [1, W]]),
                                                  view(ch, 0, 128, zo, [[CW, CZ], [1, W]]), ALU.subtract
                                                  ).then_inc(sem["zl_done"], 1)
                    elif on(j + 1):
                        dve.wait_ge(sem["zh_done"], j + 2)
                        zo = ((slot + 1) % 2) * CZ * CW + 1
                        dve.tensor_tensor(view(cl, 0, 128, zo, [[CW, CZ], [1, W]]),
                                          view(cf, 0, 128, 0, [[W, CZ], [1, W]]),
                                          view(ch, 0, 128, zo, [[CW, CZ], [1, W]]), ALU.subtract
                                          ).then_inc(sem["zl_done"], 1)
                strips(dve, body)


def kernel(x, L0_conv_W_qkv, L0_conv_W_out, L0_conv_rel_height, L0_conv_rel_width, L1_conv_weight, L1_conv_bias):
    import numpy as np
    import concourse.bacc as bacc
    from concourse.bass_utils import run_bass_kernel_spmd

    nc = bacc.Bacc("TRN2", target_bir_lowering=False, num_devices=1)
    x = np.asarray(x)
    rows = np.zeros((C, ROWS + 2 * PAD, W), x.dtype)
    rows[:, PAD:PAD + ROWS] = x.transpose(1, 0, 2, 3).reshape(C, ROWS, W)
    lo, hi = WS + 2 * PAD - WS + 1, 2 * (WS + 2 * PAD) - 2
    rel = np.concatenate([np.asarray(t)[lo:hi:2].T for t in (L0_conv_rel_height, L0_conv_rel_width)], axis=1)
    rel = np.tile(rel, (HEADS, 1))
    part = np.arange(128)
    groups = (part[:, None] // GROUP == part[None, :] // GROUP).astype(np.float32)
    shift = np.concatenate([(QS - 1 - part[:, None] % QS == np.arange(QS)),
                            (QS - 1 - (part[:, None] // QS) % QS == np.arange(QS))], axis=1).astype(np.float32)
    first = np.tile((np.arange(STRIPS) % (STRIPS // B) != 0), (128, 1))
    final = np.tile((np.arange(STRIPS) % (STRIPS // B) != STRIPS // B - 1), (128, 1))
    arrays = {
        "rows": rows,
        "wqkv": np.ascontiguousarray(np.asarray(L0_conv_W_qkv).T),
        "wout": np.ascontiguousarray(np.asarray(L0_conv_W_out).T),
        "rel": np.ascontiguousarray(rel),
        "wconv": np.ascontiguousarray(np.asarray(L1_conv_weight).transpose(1, 2, 3, 0).reshape(C, 9 * C)),
        "bias": np.ascontiguousarray(np.asarray(L1_conv_bias).reshape(C, 1)),
        "ident": np.eye(128, dtype=np.float16),
        "groups": groups,
        "heads": (part[:, None] // DH == np.arange(HEADS)).astype(np.float16),
        "shift": shift,
        "edge": np.concatenate([first, final], axis=1).astype(np.float32),
    }
    aps = [nc.dram_tensor(n, a.shape, mybir.dt.from_np(a.dtype), kind="ExternalInput").ap() for n, a in arrays.items()]
    x1 = nc.dram_tensor("x1", (C, ROWS + 2, W), F32, kind="Internal").ap()
    out = nc.dram_tensor("out", (C, ROWS, W), F32, kind="ExternalOutput").ap()
    conv_preact_program(nc, *aps, x1, out)
    got = run_bass_kernel_spmd(nc, [arrays], core_ids=[0]).results[0]["out"]
    return np.ascontiguousarray(got.reshape(C, B, H, W).transpose(1, 0, 2, 3))
```

```python
from contextlib import ExitStack

import concourse.bass as bass
from concourse import mybir

F32 = mybir.dt.float32
F16 = mybir.dt.float16
U32 = mybir.dt.uint32
ALU = mybir.AluOpType
ACT = mybir.ActivationFunctionType
AX = mybir.AxisListType
RMAX = bass.bass_isa.ReduceOp.max

B, C, H, W = 2, 128, 256, 256
HEADS, DH = 4, 32
WS, PAD = 8, 2
GROUP = C // 32
EPS = 1e-5
TILE, THRESHOLD = 32, 1e-6

PAR = 4
QS, KS = WS // 2, (WS + 2 * PAD) // 2
QN, KN = QS * QS, KS * KS
RN = QS + KS - 1
KR = KN + 2 * RN

ROWS = B * H
STRIPS = ROWS // WS
UNITS = 2 * STRIPS
UW = W // 2
NW = UW // WS
GW = 4
GROUPS = NW // GW
LC = UW + PAD
ZR = WS + 2 * PAD
PJ = (UW + 2 * PAD) // 2
PLANE = PJ * KS
QP = QS * UW // 2
KV = KS * (GW * QS + 2)
WK = KS * QS
PAIRS = 2 * GW
DSLOT = KV + WK
QB = C // 2
QBW = QB + 2 * QB * PAR * NW

CROWS = 8
CSTRIPS = ROWS // CROWS
CW = W + 2
NM = 4
TAPS = NM * 3
PAIRROWS = CROWS // 2
TC = W // TILE


def view(t, p0, p1, off, dims):
    base = t[p0:p1, 0:1]
    return bass.AP(base.tensor, base.offset + off, [list(base.ap[0])] + [list(d) for d in dims])


def settled(eng, value):
    return value if isinstance(value, int) else eng.snap(value)


def need(eng, sem, value):
    if isinstance(value, int) and value <= 0:
        return
    eng.wait_ge(sem, value)


def conv_preact_program(nc, x_in, wqkv_in, wout_in, rel_in, wconv_in, bias_in, ident_in, gsum_in,
                        heads_in, shift_in, edge_in, x1_dram, out):
    with ExitStack() as ctx:
        def sb(name, cols, dt, stack=ctx):
            return stack.enter_context(nc.sbuf_tensor(f"sb_{name}", [128, cols], dt))

        wq_h, wq_l = sb("wq_h", 3 * C, F16), sb("wq_l", 3 * C, F16)
        wo_h, wo_l = sb("wo_h", C, F16), sb("wo_l", C, F16)
        wc_h, wc_l = sb("wc_h", TAPS * C, F16), sb("wc_l", TAPS * C, F16)
        rel_h, rel_l = sb("rel_h", 2 * RN, F16), sb("rel_l", 2 * RN, F16)
        bias = sb("bias", 1, F32)
        ident = sb("ident", 128, F16)
        gsum = sb("gsum", 128, F32)
        heads = sb("heads", HEADS, F16)
        shift = sb("shift", 2 * QS, F32)
        edge = sb("edge", 2 * STRIPS, F32)
        amax = sb("amax", 3, F32)
        amax_all = sb("amax_all", 3, F32)
        wscale = sb("wscale", 3, F32)
        wneg = sb("wneg", 1, F32)
        winv = sb("winv", 3, F32)
        alpha = sb("alpha", 1, F32)
        oscale = sb("oscale", 1, F32)
        stats = sb("stats", UNITS * 2 * 6, F32)
        aggr = sb("aggr", 2 * B, F32)
        moments = sb("moments", 2 * B, F32)
        gn = [sb(f"gn{j}", B, F32) for j in range(8)]
        mean_t = sb("mean_t", STRIPS, F32)
        rstd_t = sb("rstd_t", 3 * STRIPS, F32)
        tmax = sb("tmax", UNITS * 4, F32)
        tmin = sb("tmin", UNITS * 4, F32)

        def groupnorm_moments(phase):
            agg_done, sum_done, step_done, sqrt_done = (
                ctx.enter_context(nc.semaphore(f"{phase}_{n}")) for n in ("agg_done", "sum_done", "step_done", "sqrt_done"))
            with nc.psum_tensor(f"{phase}_ps", [128, 512], F32) as ps, nc.Block() as block:
                @block.vector
                def _(dve):
                    k = 0

                    def link(ins):
                        nonlocal k
                        k += 1
                        ins.then_inc(step_done, 1)
                        dve.wait_ge(step_done, k)
                    half = UNITS * 6
                    for b in range(B):
                        link(dve.bn_aggr(aggr[:, 2 * b:2 * b + 2], stats[:, b * half:(b + 1) * half]))
                    mean = view(aggr, 0, 128, 0, [[2, B]])
                    var = view(aggr, 0, 128, 1, [[2, B]])
                    link(dve.tensor_tensor(gn[0][:], mean, mean, ALU.mult))
                    dve.tensor_tensor(var, var, gn[0][:], ALU.add).then_inc(agg_done, 1)
                    dve.wait_ge(sum_done, 1)
                    link(dve.tensor_scalar(moments[:], ps[:, 0:2 * B], 1.0 / GROUP, None, ALU.mult))
                    gmean = view(moments, 0, 128, 0, [[2, B]])
                    gsq = view(moments, 0, 128, 1, [[2, B]])
                    link(dve.tensor_tensor(gn[1][:], gmean, gmean, ALU.mult))
                    link(dve.tensor_tensor(gn[2][:], gsq, gn[1][:], ALU.subtract))
                    link(dve.tensor_scalar(gn[2][:], gn[2][:], 0.0, EPS, ALU.max, ALU.add))
                    link(dve.reciprocal(gn[3][:], gn[2][:]))
                    dve.wait_ge(sqrt_done, 1)
                    for _ in range(2):
                        link(dve.tensor_tensor(gn[4][:], gn[5][:], gn[5][:], ALU.mult))
                        link(dve.tensor_tensor(gn[4][:], gn[4][:], gn[2][:], ALU.mult))
                        link(dve.tensor_scalar(gn[4][:], gn[4][:], -0.5, 1.5, ALU.mult, ALU.add))
                        link(dve.tensor_tensor(gn[5][:], gn[5][:], gn[4][:], ALU.mult))
                    hs = STRIPS // B
                    for b in range(B):
                        link(dve.tensor_copy(mean_t[:, b * hs:(b + 1) * hs],
                                             view(moments, 0, 128, 2 * b, [[0, hs]])))
                        link(dve.tensor_copy(rstd_t[:, STRIPS + b * hs:STRIPS + (b + 1) * hs],
                                             view(gn[5], 0, 128, b, [[0, hs]])))
                    link(dve.tensor_tensor(rstd_t[:, 0:STRIPS], rstd_t[:, STRIPS:2 * STRIPS],
                                           edge[:, 0:STRIPS], ALU.mult))
                    link(dve.tensor_tensor(rstd_t[:, 2 * STRIPS:], rstd_t[:, STRIPS:2 * STRIPS],
                                           edge[:, STRIPS:], ALU.mult))

                @block.tensor
                def _(pe):
                    pe.wait_ge(agg_done, 1)
                    pe.matmul(ps[:, 0:2 * B], gsum[:], aggr[:], start=True, stop=True).then_inc(sum_done, 1)

                @block.scalar
                def _(act):
                    act.wait_ge(step_done, 8)
                    act.activation(gn[5][:], gn[3][:], ACT.Sqrt).then_inc(sqrt_done, 1)

        A_ROWS, A_RING = 16, 4
        A_TILES = ROWS // A_ROWS
        with ExitStack() as pa:
            raw = sb("raw", 3 * C + 2 * RN + C + 9 * C, F32, pa)
            rawn = sb("rawn", 3 * C + 2 * RN + C + 9 * C, F32, pa)
            gw = sb("gw", TAPS * C + 3 * C, F32, pa)
            abuf = sb("abuf", A_RING * A_ROWS * W, F32, pa)
            w_loaded = ctx.enter_context(nc.semaphore("w_loaded"))
            x_loaded = [ctx.enter_context(nc.semaphore(f"a_x_loaded{r}")) for r in range(A_RING)]
            x_used = ctx.enter_context(nc.semaphore("a_x_used"))
            max_done = ctx.enter_context(nc.semaphore("w_max_done"))
            all_done = ctx.enter_context(nc.semaphore("w_all_done"))
            w_step = ctx.enter_context(nc.semaphore("w_step"))
            w_hi = ctx.enter_context(nc.semaphore("w_hi"))
            w_norm = ctx.enter_context(nc.semaphore("w_norm"))
            SPANS = [(0, 3 * C + 2 * RN), (3 * C + 2 * RN, 4 * C + 2 * RN), (4 * C + 2 * RN, 13 * C + 2 * RN)]
            PARTS = [(0, 3 * C, wq_h, wq_l), (3 * C, 3 * C + 2 * RN, rel_h, rel_l),
                     (SPANS[1][0], SPANS[1][1], wo_h, wo_l)]
            with nc.Block() as block:
                @block.sync
                def _(sp):
                    sp.dma_start(raw[:, 0:3 * C], wqkv_in).then_inc(w_loaded, 16)
                    sp.dma_start(raw[:, 3 * C:3 * C + 2 * RN], rel_in).then_inc(w_loaded, 16)
                    sp.dma_start(raw[:, SPANS[1][0]:SPANS[1][1]], wout_in).then_inc(w_loaded, 16)
                    sp.dma_start(raw[:, SPANS[2][0]:SPANS[2][1]], wconv_in).then_inc(w_loaded, 16)
                    sp.dma_start(bias[:], bias_in).then_inc(w_loaded, 16)
                    sp.dma_start(ident[:], ident_in).then_inc(w_loaded, 16)
                    sp.dma_start(gsum[:], gsum_in).then_inc(w_loaded, 16)
                    sp.dma_start(heads[:], heads_in).then_inc(w_loaded, 16)
                    sp.dma_start(shift[:], shift_in).then_inc(w_loaded, 16)
                    sp.dma_start(edge[:], edge_in).then_inc(w_loaded, 16)

                    def load(row, r):
                        sp.dma_start(abuf[:, r * A_ROWS * W:(r + 1) * A_ROWS * W],
                                     x_in[:, bass.ds(row, A_ROWS), :]
                                     .rearrange("p a b -> p (a b)")).then_inc(x_loaded[r], 16)
                    for r in range(A_RING):
                        load(r * A_ROWS + PAD, r)
                    with sp.Fori(0, A_TILES // A_RING - 1) as i:
                        for r in range(A_RING):
                            row = sp.snap((i * A_RING + (A_RING + r)) * A_ROWS + PAD)
                            sp.wait_ge(x_used, i * A_RING + r + 1)
                            load(row, r)

                @block.vector
                def _(dve):
                    dve.wait_ge(w_loaded, 10 * 16)
                    for j, (a, b) in enumerate(SPANS):
                        last = dve.tensor_reduce(amax[:, j:j + 1], raw[:, a:b], AX.X, ALU.max,
                                                 apply_absolute_value=True)
                    last.then_inc(max_done, 1)
                    dve.wait_ge(all_done, 1)
                    dve.tensor_scalar(amax_all[:], amax_all[:], 1e-30, None, ALU.max).then_inc(w_step, 1)
                    dve.wait_ge(w_step, 1)
                    dve.tensor_scalar(wscale[:].bitcast(U32), amax_all[:].bitcast(U32), 0x7F800000, None,
                                      ALU.bitwise_and).then_inc(w_step, 1)
                    dve.wait_ge(w_step, 2)
                    dve.reciprocal(winv[:], wscale[:]).then_inc(w_step, 1)
                    dve.tensor_scalar(alpha[:], wscale[:, 0:1], wscale[:, 0:1], DH ** -0.5, ALU.mult,
                                      ALU.mult).then_inc(w_step, 1)
                    dve.tensor_tensor(oscale[:], wscale[:, 0:1], wscale[:, 1:2], ALU.mult).then_inc(w_step, 1)
                    dve.wait_ge(w_step, 5)
                    for j, (a, b) in enumerate(SPANS):
                        last = dve.tensor_scalar(rawn[:, a:b], raw[:, a:b], winv[:, j:j + 1], None, ALU.mult)
                    last.then_inc(w_norm, 1)
                    dve.wait_ge(w_norm, 1)
                    kw = [rawn[:, SPANS[2][0] + ky * 3 * C:SPANS[2][0] + (ky + 1) * 3 * C] for ky in range(3)]
                    gm = [gw[:, m * 3 * C:(m + 1) * 3 * C] for m in range(NM + 1)]
                    dve.tensor_scalar(wneg[:], wscale[:, 2:3], -1.0, None, ALU.mult)
                    dve.tensor_copy(gm[0], kw[0])
                    dve.tensor_copy(gm[3], kw[2])
                    dve.tensor_tensor(gm[4], kw[0], kw[2], ALU.add).then_inc(w_norm, 1)
                    dve.wait_ge(w_norm, 2)
                    dve.tensor_scalar(gm[4], gm[4], 0.5, None, ALU.mult).then_inc(w_norm, 1)
                    dve.wait_ge(w_norm, 3)
                    dve.scalar_tensor_tensor(gm[1], kw[1], 0.5, gm[4], ALU.mult, ALU.add)
                    dve.scalar_tensor_tensor(gm[2], kw[1], -0.5, gm[4], ALU.mult, ALU.add).then_inc(w_norm, 1)
                    dve.wait_ge(w_norm, 4)
                    dve.tensor_copy(wc_h[:], gw[:, 0:TAPS * C]).then_inc(w_hi, 1)
                    for a, b, hi, _ in PARTS:
                        dve.tensor_copy(hi[:], rawn[:, a:b]).then_inc(w_hi, 1)
                    dve.wait_ge(w_hi, len(PARTS) + 1)
                    dve.tensor_tensor(wc_l[:], gw[:, 0:TAPS * C], wc_h[:], ALU.subtract)
                    for a, b, hi, lo in PARTS:
                        dve.tensor_tensor(lo[:], rawn[:, a:b], hi[:], ALU.subtract)
                    with dve.Fori(0, A_TILES // A_RING) as i:
                        for r in range(A_RING):
                            dve.wait_ge(x_loaded[r], i * 16 + 16)
                            for c in range(A_ROWS * W // 512):
                                last = dve.bn_stats(
                                    stats[:, bass.ds(i * (A_RING * A_ROWS * W // 512 * 6)
                                                     + (r * A_ROWS * W // 512 + c) * 6, 6)],
                                    abuf[:, r * A_ROWS * W + c * 512:r * A_ROWS * W + (c + 1) * 512])
                            last.then_inc(x_used, 1)

                @block.gpsimd
                def _(pool):
                    pool.wait_ge(max_done, 1)
                    pool.partition_all_reduce(amax_all[:], amax[:], 128, RMAX).then_inc(all_done, 1)
            groupnorm_moments("gn0")

        with ExitStack() as pb:
            names = ("zf_done", "zh_done", "zl0_done", "zl1_done", "q_mm", "qh_done", "ql_done",
                     "k_mm", "kh_done", "kl_done", "qbh_done", "qbl_done", "s_mm", "rel_out", "prod_done", "b_done", "e_done",
                     "s2_done", "max_done", "sub_done", "exp_done", "sum_done", "rcp_done", "norm_done",
                     "ph_done", "pl_done", "t_mm", "pt0_done", "pt1_done", "v_mm", "vh_done", "vl_done",
                     "o_mm", "ext_done", "oh_done", "ol_done", "y_mm", "x1_done", "x1_read", "x1_stored",
                     "zeroed")
            sem = {n: pb.enter_context(nc.semaphore(f"b_{n}")) for n in names}
            x_loaded, xr_loaded = ([pb.enter_context(nc.semaphore(f"b_{n}{h}")) for h in range(2)]
                                   for n in ("x_loaded", "xr_loaded"))
            xb = sb("xb", 2 * ZR * LC, F32, pb)
            zf = sb("zf", ZR * LC, F32, pb)
            zh, zl = sb("zh", 4 * PAR * PLANE, F16, pb), sb("zl", 4 * PAR * PLANE, F16, pb)
            qh, ql = sb("qh", PAR * QP, F16, pb), sb("ql", PAR * QP, F16, pb)
            KU = PAR * NW * KR
            kh, kl = sb("kh", 2 * KU, F16, pb), sb("kl", 2 * KU, F16, pb)
            qbh, qbl = sb("qbh", 2 * QBW, F16, pb), sb("qbl", 2 * QBW, F16, pb)
            NS = PAIRS * KN
            rel = sb("rel", 2 * PAIRS * 2 * RN, F32, pb)
            prod = sb("prod", 2 * PAIRS * KS * QS, F32, pb)
            brel = sb("brel", 2 * PAIRS * KS, F32, pb)
            erel = sb("erel", NS, F32, pb)
            sp_ = sb("scores", 2 * NS, F32, pb)
            smax = sb("smax", 2 * PAIRS, F32, pb)
            ssum = sb("ssum", 2 * PAIRS, F32, pb)
            srcp = sb("srcp", 2 * PAIRS, F32, pb)
            DB = PAIRS * DSLOT
            dh, dl = sb("dh", 2 * DB, F16, pb), sb("dl", 2 * DB, F16, pb)
            pt = sb("pt", 2 * 2048, F16, pb)
            vh, vl = sb("vh", 2 * 512, F16, pb), sb("vl", 2 * 512, F16, pb)
            of = sb("of", 2 * 256, F32, pb)
            oh, ol = sb("oh", 2 * 1024, F16, pb), sb("ol", 2 * 1024, F16, pb)
            x1 = sb("x1", 2 * WS * UW, F32, pb)

            def ps(name, cols=512, dt=F32):
                return pb.enter_context(nc.psum_tensor(name, [128, cols], dt))
            ps_q, ps_k, ps_v = ps("ps_q"), ps("ps_k"), ps("ps_v")
            ps_s = [ps("ps_s0"), ps("ps_s1")]
            ps_t = ps("ps_t", 1024, F16)
            ps_o = ps("ps_o", 1024)

            FIRST, LOOP = 6, 4
            TURNS = (UNITS - 3 - FIRST) // LOOP
            GT = UNITS * GROUPS

            def units(eng, body):
                for u in range(-3, FIRST):
                    body(u, u // 2, u % 4, lambda v, top: 0 <= v < top)
                with eng.Fori(0, TURNS) as i:
                    for c in range(LOOP):
                        body(i * LOOP + (FIRST + c), i * (LOOP // 2) + (FIRST + c) // 2, (FIRST + c) % 4,
                             lambda v, top: True)
                for u in range(FIRST + LOOP * TURNS, UNITS + 4):
                    body(u, u // 2, u % 4, lambda v, top: 0 <= v < top)

            def z_plane(t, slot, p, off, dims, p1=128):
                return view(t, 0, p1, (slot % 4) * PAR * PLANE + p * PLANE + off, dims)

            def low_rows(eng, u, h, slot, py):
                eng.wait_ge(sem["zh_done"], u + 3)
                dims = [[PLANE, 2], [KS, LC // 2], [1, KS]]
                off = ((slot + 2) % 4) * PAR * PLANE + 2 * py * PLANE + (1 - h) * KS
                eng.tensor_tensor(view(zl, 0, 128, off, dims),
                                  view(zf, 0, 128, py * LC, [[1, 2], [2, LC // 2], [2 * LC, KS]]),
                                  view(zh, 0, 128, off, dims), ALU.subtract).then_inc(sem[f"zl{py}_done"], 1)

            block = pb.enter_context(nc.Block())

            @block.sync
            def _(sp):
                def body(u, s, slot, on):
                    h = slot % 2
                    if on(u + 3, UNITS):
                        row = settled(sp, (s + (h + 3) // 2) * WS)
                        need(sp, sem["zf_done"], u + 2)
                        r = (slot + 3) % 2
                        sp.dma_start(view(xb, 0, 128, r * ZR * LC, [[LC, ZR], [1, LC]]),
                                     x_in[:, bass.ds(row, ZR),
                                          (UW - PAD) * r:(UW - PAD) * r + LC]).then_inc(x_loaded[r], 16)
                    if on(u - 3, UNITS):
                        row = settled(sp, (s - 1 - (1 - h)) * WS + 1)
                        sp.wait_ge(sem["x1_done"], (u - 2) * PAR)
                        sp.dma_start(x1_dram[:, bass.ds(row, WS), UW * (1 - h):UW * (1 - h) + UW],
                                     view(x1, 0, 128, (1 - h) * WS * UW, [[UW, WS], [1, UW]])
                                     ).then_inc(sem["x1_stored"], 16)
                    if on(u - 1, UNITS):
                        row = settled(sp, (s + (h - 1) // 2) * WS + PAD)
                        done = settled(sp, (u - 2) * 16)
                        need(sp, sem["x1_read"], done)
                        need(sp, sem["x1_stored"], done)
                        r = (slot + 3) % 2
                        sp.dma_start(view(x1, 0, 128, r * WS * UW, [[UW, WS], [1, UW]]),
                                     x_in[:, bass.ds(row, WS),
                                          UW * r:UW * r + UW]).then_inc(xr_loaded[r], 16)
                units(sp, body)
                sp.wait_ge(sem["x1_stored"], UNITS * 16)

            @block.tensor
            def _(pe):
                def project(p, slot, u, side):
                    piece = u * PAR + p
                    if p == 0:
                        pe.wait_ge(sem["zl0_done"], u + 1)
                        pe.wait_ge(sem["zl1_done"], u + 1)
                    need(pe, sem["ql_done"], piece)
                    if p in Y_BEFORE:
                        need(pe, sem["x1_done"], Y_BEFORE[p] + (u - 3) * PAR)
                    dq = [[KS, UW // 2], [1, QS]]
                    q_at = lambda z: z_plane(z, slot, p, KS + 1, dq)
                    pe.matmul(ps_q[:, 0:QP], wq_h[:, 0:C], q_at(zh), start=True, stop=False)
                    pe.matmul(ps_q[:, 0:QP], wq_h[:, 0:C], q_at(zl), start=False, stop=False)
                    pe.matmul(ps_q[:, 0:QP], wq_l[:, 0:C], q_at(zh), start=False, stop=True).then_inc(sem["q_mm"], 1)
                    need(pe, sem["kl_done"], piece)
                    k_at = lambda z: z_plane(z, slot, p, 0, [[1, PLANE]])
                    pe.matmul(ps_k[:, 0:PLANE], wq_h[:, C:2 * C], k_at(zh), start=True, stop=False)
                    pe.matmul(ps_k[:, 0:PLANE], wq_h[:, C:2 * C], k_at(zl), start=False, stop=False)
                    pe.matmul(ps_k[:, 0:PLANE], wq_l[:, C:2 * C], k_at(zh), start=False,
                              stop=True).then_inc(sem["k_mm"], 1)

                def transposes(m, par, py):
                    if py == 0:
                        pe.wait_ge(sem["pl_done"], m + 1)
                        need(pe, sem["pt1_done"], m)
                    else:
                        pe.wait_ge(sem["pt0_done"], m + 1)
                    for wj in range(GW):
                        pr = py * GW + wj
                        at = pr * DSLOT - WK * wj
                        for part, d in enumerate((dh, dl)):
                            last = pe.transpose(ps_t[0:KV, (2 * wj + part) * 128:(2 * wj + part + 1) * 128],
                                                d[:, par * DB + at:par * DB + at + KV], ident[:])
                    last.then_inc(sem["t_mm"], 1)

                def body(u, s, slot, on):
                    for g in range(GROUPS):
                        n = u * GROUPS + g
                        if on(n, GT):
                            if g == 0:
                                pe.wait_ge(sem["qbh_done"], u + 1)
                                pe.wait_ge(sem["qbl_done"], u + 1)
                                pe.wait_ge(sem["kl_done"], (u + 1) * PAR)
                            need(pe, sem["s2_done"], n - 1)
                            ub = slot % 2
                            for pr in range(PAIRS):
                                py, wj = divmod(pr, GW)
                                s_at = ps_s[g % 2][:, pr * KR:(pr + 1) * KR]
                                for px in range(2):
                                    p, w = 2 * py + px, GW * g + wj
                                    qc = ub * QBW + (p * NW + w) * 2 * QB + (QB if px == 0 else 0)
                                    kc = ub * KU + (p * NW + w) * KR
                                    terms = ((qbh, kh), (qbh, kl), (qbl, kh))
                                    for t, (q, k) in enumerate(terms):
                                        last = pe.matmul(s_at, q[:, qc:qc + 2 * QB], k[:, kc:kc + KR],
                                                         start=(px == 0 and t == 0), stop=(px == 1 and t == 2))
                            last.then_inc(sem["s_mm"], 1)
                        if g == 1 and on(u + 1, UNITS):
                            project(2 * g, slot + 1, u + 1, (slot + 1) % 2)
                        if on(n - 3, GT):
                            transposes(n - 3, (g - 3) % 2, 0)
                        if on(n - 3, GT):
                            m = n - 3
                            vslot, vg = (slot, 0) if g == 3 else (slot - 1, g + 1)
                            need(pe, sem["vl_done"], m)
                            for p in range(PAR):
                                z_at = lambda z: z_plane(z, vslot, p, GW * WK * vg, [[1, KV]])
                                v_out = ps_v[0:KV, p * C:(p + 1) * C]
                                pe.matmul(v_out, z_at(zh), wq_h[:, 2 * C:3 * C], start=True, stop=False)
                                pe.matmul(v_out, z_at(zh), wq_l[:, 2 * C:3 * C], start=False, stop=False)
                                last = pe.matmul(v_out, z_at(zl), wq_h[:, 2 * C:3 * C], start=False, stop=True)
                            last.then_inc(sem["v_mm"], 1)
                        if g == 0 and on(u + 1, UNITS):
                            project(0, slot + 1, u + 1, (slot + 1) % 2)
                        if on(n - 4, GT):
                            m, par = n - 4, g % 2
                            pe.wait_ge(sem["pt1_done"], m + 1)
                            pe.wait_ge(sem["vl_done"], m + 1)
                            need(pe, sem["ext_done"], m)
                            for p in range(PAR):
                                py, px = divmod(p, 2)
                                o_at = ps_o[:, p * 256:(p + 1) * 256]
                                v_at = lambda v: v[0:KV, par * 512 + p * C:par * 512 + (p + 1) * C]
                                p_at = lambda part: view(pt, 0, KV, par * 2048 + py * 1024 + part * 128 + px * 64,
                                                         [[256, GW], [1, QB]])
                                pe.matmul(o_at, v_at(vh), p_at(0), start=True, stop=False)
                                pe.matmul(o_at, v_at(vh), p_at(1), start=False, stop=False)
                                last = pe.matmul(o_at, v_at(vl), p_at(0), start=False, stop=True)
                            last.then_inc(sem["o_mm"], 1)
                        if on(n - 3, GT):
                            transposes(n - 3, (g - 3) % 2, 1)
                        if g < 2 and on(u + 1, UNITS):
                            project(2 * g + 1, slot + 1, u + 1, (slot + 1) % 2)
                        if on(u - 2, UNITS):
                            piece = (u - 2) * PAR + g
                            if g == 0:
                                pe.wait_ge(sem["ol_done"], (u - 1) * GROUPS)
                            if g < 2:
                                need(pe, sem["ql_done"], QL_BEFORE(u, g))
                            need(pe, sem["x1_done"], piece)
                            ob = slot % 2
                            o_rhs = lambda o: o[:, ob * 1024 + g * QP:ob * 1024 + (g + 1) * QP]
                            pe.matmul(ps_q[:, 0:QP], wo_h[:], o_rhs(oh), start=True, stop=False)
                            pe.matmul(ps_q[:, 0:QP], wo_h[:], o_rhs(ol), start=False, stop=False)
                            pe.matmul(ps_q[:, 0:QP], wo_l[:], o_rhs(oh), start=False, stop=True
                                      ).then_inc(sem["y_mm"], 1)
                Y_BEFORE = {0: 0, 2: 1}

                def QL_BEFORE(u, g):
                    if not isinstance(u, int):
                        return (u + 1) * PAR + 2 * g + 2
                    return min((u + 1) * PAR + 2 * g + 2, UNITS * PAR)
                pe.wait_ge(sem["zeroed"], 3)
                units(pe, body)

            @block.vector
            def _(dve):
                for t in (zh, zl):
                    for slot in range(4):
                        last = dve.memset(view(t, 0, 128, slot * PAR * PLANE + (slot % 2) * (PJ - 1) * KS,
                                               [[PLANE, PAR], [1, KS]]), 0.0)
                for t in (dh, dl):
                    last = dve.memset(t[:], 0.0)
                for t, src in ((kh, rel_h), (kl, rel_l)):
                    for b in range(2):
                        last = dve.tensor_copy(view(t, 0, 128, b * KU + KN, [[KR, PAR * NW], [1, 2 * RN]]),
                                               view(src, 0, 128, 0, [[0, PAR * NW], [1, 2 * RN]]))
                last.then_inc(sem["zeroed"], 1)

                def low_queries(u, p):
                    piece = (u + 1) * PAR + p
                    if p == 0:
                        need(dve, sem["qbl_done"], u + 1)
                    dve.wait_ge(sem["qh_done"], piece + 1)
                    dve.tensor_tensor(ql[:, p * QP:(p + 1) * QP], ps_q[:, 0:QP],
                                      qh[:, p * QP:(p + 1) * QP], ALU.subtract).then_inc(sem["ql_done"], 1)

                def low_keys(u, h, p):
                    piece = (u + 1) * PAR + p
                    dve.wait_ge(sem["kh_done"], piece + 1)
                    k_off = (1 - h) * KU + p * NW * KR
                    k_dims = [[KR, NW], [1, KN]]
                    dve.tensor_tensor(view(kl, 0, 128, k_off, k_dims),
                                      view(ps_k, 0, 128, 0, [[WK, NW], [1, KN]]),
                                      view(kh, 0, 128, k_off, k_dims), ALU.subtract).then_inc(sem["kl_done"], 1)

                def body(u, s, slot, on):
                    h = slot % 2
                    for g in range(GROUPS):
                        n = u * GROUPS + g
                        b0 = g % 2
                        b1 = 1 - b0
                        nn = slice(b0 * NS, (b0 + 1) * NS)
                        n8 = slice(b0 * PAIRS, (b0 + 1) * PAIRS)
                        by_pair = lambda t, b: view(t, 0, 128, b * NS, [[KN, PAIRS], [1, KN]])
                        if on(u - 2 if g else u - 3, UNITS):
                            xu, xp, xh = (u - 2, g - 1, h) if g else (u - 3, PAR - 1, 1 - h)
                            if xp == 0:
                                dve.wait_ge(xr_loaded[h], s * 16)
                            dve.wait_ge(sem["y_mm"], xu * PAR + xp + 1)
                            off = xh * WS * UW + (xp // 2) * UW + xp % 2
                            dims = [[2 * UW, QS], [2, UW // 2]]
                            dve.scalar_tensor_tensor(view(x1, 0, 128, off, dims),
                                                     view(ps_q, 0, 128, 0, [[1, QS], [QS, UW // 2]]),
                                                     oscale[:, 0:1], view(x1, 0, 128, off, dims), ALU.mult, ALU.add
                                                     ).then_inc(sem["x1_done"], 1)
                        if on(n - 1, GT):
                            dve.wait_ge(sem["prod_done"], n)
                            dve.tensor_reduce(brel[:], view(prod, 0, 128, 0, [[QS, 2 * PAIRS * KS], [1, QS]]),
                                              AX.X, ALU.add).then_inc(sem["b_done"], 1)
                        if on(n - 2, GT):
                            dve.wait_ge(sem["exp_done"], n - 1)
                            dve.tensor_reduce(ssum[:, n8], by_pair(sp_, b0), AX.X, ALU.add
                                              ).then_inc(sem["sum_done"], 1)
                        if on(n, GT):
                            dve.wait_ge(sem["s_mm"], n + 1)
                            need(dve, sem["prod_done"], n - 1)
                            dve.tensor_copy(view(rel, 0, 128, b0 * PAIRS * 2 * RN, [[2 * RN, PAIRS], [1, 2 * RN]]),
                                            view(ps_s[g % 2], 0, 128, KN, [[KR, PAIRS], [1, 2 * RN]])
                                            ).then_inc(sem["rel_out"], 1)
                        if on(n - 2, GT):
                            dve.wait_ge(sem["sum_done"], n - 1)
                            need(dve, sem["norm_done"], n - 3)
                            dve.reciprocal(srcp[:, n8], ssum[:, n8]).then_inc(sem["rcp_done"], 1)
                        if g == 0 and on(u - 3, UNITS):
                            dve.wait_ge(sem["x1_done"], (u - 2) * PAR)
                            for c in range(2):
                                dve.bn_stats(stats[:, bass.ds((u - 3) * 12 + c * 6, 6)],
                                             x1[:, (1 - h) * WS * UW + c * 512:(1 - h) * WS * UW + (c + 1) * 512])
                        if g >= 2 and on(u + 1, UNITS):
                            if g == 2:
                                need(dve, sem["s_mm"], u * GROUPS)
                                dve.wait_ge(sem["qh_done"], (u + 2) * PAR)
                            else:
                                dve.wait_ge(sem["ql_done"], (u + 2) * PAR)
                            src, dst, done = (qh, qbh, "qbh_done") if g == 2 else (ql, qbl, "qbl_done")
                            for hd in range(HEADS):
                                last = dve.tensor_copy(view(dst, DH * hd, DH * hd + DH, (1 - h) * QBW + QB + hd * QN,
                                                            [[2 * QB, PAR * NW], [1, QN]]),
                                                       view(src, DH * hd, DH * hd + DH, 0, [[QN, PAR * NW], [1, QN]]))
                            last.then_inc(sem[done], 1)
                        if g == 3 and on(u + 2, UNITS):
                            low_rows(dve, u, h, slot, 1)
                        if on(n - 1, GT):
                            dve.wait_ge(sem["e_done"], n)
                            need(dve, sem["pl_done"], n - 2)
                            dve.tensor_tensor(by_pair(sp_, b1), view(ps_s[1 - g % 2], 0, 128, 0, [[KR, PAIRS], [1, KN]]),
                                              view(erel, 0, 128, 0, [[KN, PAIRS], [1, KN]]), ALU.add
                                              ).then_inc(sem["s2_done"], 1)
                        if on(n - 1, GT):
                            dve.wait_ge(sem["s2_done"], n)
                            need(dve, sem["sub_done"], n - 2)
                            dve.tensor_reduce(smax[:, b1 * PAIRS:(b1 + 1) * PAIRS], by_pair(sp_, b1), AX.X, ALU.max
                                              ).then_inc(sem["max_done"], 1)
                        if g < 2 and on(u + 1, UNITS):
                            low_queries(u, 2 * g)
                        if g == 1 and on(u + 2, UNITS):
                            dve.wait_ge(x_loaded[h], (s + 2) * 16)
                            need(dve, sem["zl0_done"], u + 2)
                            need(dve, sem["zl1_done"], u + 2)
                            s2_ = s + 1
                            for part, (r0, r1) in enumerate(((0, PAD), (PAD, ZR - PAD), (ZR - PAD, ZR))):
                                last = dve.tensor_scalar(zf[:, r0 * LC:r1 * LC],
                                                         xb[:, (h * ZR + r0) * LC:(h * ZR + r1) * LC],
                                                         mean_t[:, bass.ds(s2_, 1)],
                                                         rstd_t[:, bass.ds(s2_ + part * STRIPS, 1)],
                                                         ALU.subtract, ALU.mult)
                            last.then_inc(sem["zf_done"], 1)
                        if g < 2 and on(u + 1, UNITS):
                            low_keys(u, h, 2 * g)
                        if g >= 2 and on(u - 3, UNITS):
                            t, op = (tmax, ALU.max) if g == 2 else (tmin, ALU.min)
                            last = dve.tensor_reduce(t[:, bass.ds((u - 3) * 4, 4)],
                                              view(x1, 0, 128, (1 - h) * WS * UW, [[TILE, 4], [UW, WS], [1, TILE]]),
                                              AX.XY, op)
                            if g == 3:
                                last.then_inc(sem["x1_read"], 16)
                        if g < 2 and on(u + 1, UNITS):
                            low_queries(u, 2 * g + 1)
                        if on(n - 3, GT):
                            dve.wait_ge(sem["vh_done"], n - 2)
                            dve.tensor_tensor(vl[0:KV, b1 * 512:(b1 + 1) * 512], ps_v[0:KV, :],
                                              vh[0:KV, b1 * 512:(b1 + 1) * 512], ALU.subtract
                                              ).then_inc(sem["vl_done"], 1)
                        if g < 2 and on(u + 1, UNITS):
                            low_keys(u, h, 2 * g + 1)
                dve.wait_ge(sem["zeroed"], 3)
                units(dve, body)

            @block.scalar
            def _(act):
                def high_parts(u, h, p):
                    piece = (u + 1) * PAR + p
                    if p == 0:
                        need(act, sem["qbh_done"], u + 1)
                    act.wait_ge(sem["q_mm"], piece + 1)
                    act.copy(qh[:, p * QP:(p + 1) * QP], ps_q[:, 0:QP]).then_inc(sem["qh_done"], 1)
                    if p == 0:
                        need(act, sem["s_mm"], u * GROUPS)
                    act.wait_ge(sem["k_mm"], piece + 1)
                    act.copy(view(kh, 0, 128, (1 - h) * KU + p * NW * KR, [[KR, NW], [1, KN]]),
                             view(ps_k, 0, 128, 0, [[WK, NW], [1, KN]])).then_inc(sem["kh_done"], 1)

                def body(u, s, slot, on):
                    h = slot % 2
                    for g in range(GROUPS):
                        n = u * GROUPS + g
                        b0, b1 = g % 2, 1 - g % 2
                        if on(n - 2, GT):
                            act.wait_ge(sem["sub_done"], n - 1)
                            act.activation(sp_[:, b0 * NS:(b0 + 1) * NS], sp_[:, b0 * NS:(b0 + 1) * NS], ACT.Exp,
                                           scale=alpha[:, 0:1]).then_inc(sem["exp_done"], 1)
                        if g == 2 and on(u + 2, UNITS):
                            act.wait_ge(sem["zf_done"], u + 3)
                            need(act, sem["v_mm"], (u - 1) * GROUPS)
                            for py in range(2):
                                off = ((slot + 2) % 4) * PAR * PLANE + 2 * py * PLANE + (1 - h) * KS
                                last = act.copy(view(zh, 0, 128, off, [[PLANE, 2], [KS, LC // 2], [1, KS]]),
                                                view(zf, 0, 128, py * LC, [[1, 2], [2, LC // 2], [2 * LC, KS]]))
                            last.then_inc(sem["zh_done"], 1)
                        if g < 2 and on(u + 1, UNITS):
                            high_parts(u, h, 2 * g)
                        if on(n - 3, GT):
                            act.wait_ge(sem["t_mm"], 2 * (n - 3) + 1)
                            need(act, sem["o_mm"], n - 4)
                            act.copy(pt[0:KV, b1 * 2048:b1 * 2048 + 1024], ps_t[0:KV, :]
                                     ).then_inc(sem["pt0_done"], 1)
                        if on(n - 2, GT):
                            act.wait_ge(sem["norm_done"], n - 1)
                            need(act, sem["t_mm"], 2 * (n - 3))
                            need(act, sem["pl_done"], n - 3)
                            act.copy(view(dh, 0, 128, b0 * DB, [[DSLOT, PAIRS], [1, KN]]),
                                     view(sp_, 0, 128, b0 * NS, [[KN, PAIRS], [1, KN]])
                                     ).then_inc(sem["ph_done"], 1)
                        if on(n - 3, GT):
                            act.wait_ge(sem["v_mm"], n - 2)
                            need(act, sem["o_mm"], n - 4)
                            act.copy(vh[0:KV, b1 * 512:(b1 + 1) * 512], ps_v[0:KV, :]).then_inc(sem["vh_done"], 1)
                        if on(n - 4, GT):
                            act.wait_ge(sem["o_mm"], n - 3)
                            need(act, sem["ol_done"], n - 5)
                            for hd in range(HEADS):
                                last = act.copy(view(of, DH * hd, DH * hd + DH, b0 * 256, [[QN, PAR * GW], [1, QN]]),
                                                view(ps_o, DH * hd, DH * hd + DH, hd * QN, [[QB, PAR * GW], [1, QN]]))
                            last.then_inc(sem["ext_done"], 1)
                        if g < 2 and on(u + 1, UNITS):
                            high_parts(u, h, 2 * g + 1)
                        if on(n - 3, GT):
                            act.wait_ge(sem["t_mm"], 2 * (n - 2))
                            act.copy(pt[0:KV, b1 * 2048 + 1024:b1 * 2048 + 2048], ps_t[0:KV, :]
                                     ).then_inc(sem["pt1_done"], 1)
                        if on(n - 4, GT):
                            act.wait_ge(sem["ext_done"], n - 3)
                            need(act, sem["y_mm"], (u - 2) * PAR)
                            act.copy(view(oh, 0, 128, ((slot - 1) % 2) * 1024 + g * GW * QN,
                                          [[QP, PAR], [1, GW * QN]]),
                                     view(of, 0, 128, b0 * 256, [[GW * QN, PAR], [1, GW * QN]])
                                     ).then_inc(sem["oh_done"], 1)
                act.wait_ge(sem["zeroed"], 3)
                units(act, body)

            @block.gpsimd
            def _(pool):
                for t in (qbh, qbl):
                    pool.memset(t[:], 0.0).then_inc(sem["zeroed"], 1)
                pool.wait_ge(sem["zeroed"], 3)

                def body(u, s, slot, on):
                    h = slot % 2
                    for g in range(GROUPS):
                        n = u * GROUPS + g
                        b0, b1 = g % 2, 1 - g % 2
                        if on(n - 1, GT):
                            pool.wait_ge(sem["b_done"], n)
                            need(pool, sem["s2_done"], n - 1)
                            pool.tensor_tensor(view(erel, 0, 128, 0, [[KN, PAIRS], [KS, KS], [1, KS]]),
                                               view(brel, 0, 128, 0, [[KS, PAIRS], [0, KS], [1, KS]]),
                                               view(brel, 0, 128, PAIRS * KS, [[KS, PAIRS], [1, KS], [0, KS]]),
                                               ALU.add).then_inc(sem["e_done"], 1)
                        if on(n - 2, GT):
                            pool.wait_ge(sem["rcp_done"], n - 1)
                            pool.tensor_tensor(view(sp_, 0, 128, b0 * NS, [[KN, PAIRS], [1, KN]]),
                                               view(sp_, 0, 128, b0 * NS, [[KN, PAIRS], [1, KN]]),
                                               view(srcp, 0, 128, b0 * PAIRS, [[1, PAIRS], [0, KN]]), ALU.mult
                                              ).then_inc(sem["norm_done"], 1)
                        if on(n, GT):
                            pool.wait_ge(sem["rel_out"], n + 1)
                            need(pool, sem["b_done"], n)
                            for ax in range(2):
                                last = pool.tensor_tensor(
                                    view(prod, 0, 128, ax * PAIRS * KS * QS, [[KS * QS, PAIRS], [QS, KS], [1, QS]]),
                                    view(rel, 0, 128, b0 * PAIRS * 2 * RN + ax * RN, [[2 * RN, PAIRS], [1, KS], [1, QS]]),
                                    view(shift, 0, 128, ax * QS, [[0, PAIRS], [0, KS], [1, QS]]), ALU.mult)
                            last.then_inc(sem["prod_done"], 1)
                        if on(n - 1, GT):
                            pool.wait_ge(sem["max_done"], n)
                            pool.tensor_tensor(view(sp_, 0, 128, b1 * NS, [[KN, PAIRS], [1, KN]]),
                                               view(sp_, 0, 128, b1 * NS, [[KN, PAIRS], [1, KN]]),
                                               view(smax, 0, 128, b1 * PAIRS, [[1, PAIRS], [0, KN]]),
                                               ALU.subtract).then_inc(sem["sub_done"], 1)
                        if on(n - 2, GT):
                            pool.wait_ge(sem["ph_done"], n - 1)
                            d_dims = [[DSLOT, PAIRS], [1, KN]]
                            pool.tensor_tensor(view(dl, 0, 128, b0 * DB, d_dims),
                                              view(sp_, 0, 128, b0 * NS, [[KN, PAIRS], [1, KN]]),
                                              view(dh, 0, 128, b0 * DB, d_dims), ALU.subtract
                                              ).then_inc(sem["pl_done"], 1)
                        if on(n - 5, GT):
                            pool.wait_ge(sem["oh_done"], n - 4)
                            ob = (slot - (1 if g else 2)) % 2
                            og = (g - 5) % 4
                            o_dims, o_off = [[QP, PAR], [1, GW * QN]], ob * 1024 + og * GW * QN
                            pool.tensor_tensor(view(ol, 0, 128, o_off, o_dims),
                                               view(of, 0, 128, b1 * 256, [[GW * QN, PAR], [1, GW * QN]]),
                                               view(oh, 0, 128, o_off, o_dims), ALU.subtract
                                               ).then_inc(sem["ol_done"], 1)
                        if g == 2 and on(u + 2, UNITS):
                            low_rows(pool, u, h, slot, 0)
                units(pool, body)
        groupnorm_moments("gn1")

        ctab = sb("ctab", 3 * CSTRIPS * TC, F32)
        TR = ROWS // TILE
        SPT = TILE // CROWS
        with ExitStack() as pf:
            ext = [sb(f"tile_ext{j}", TR * TC, F32, pf) for j in range(2)]
            tabs = sb("tile_abs", TR * TC, F32, pf)
            f_step = ctx.enter_context(nc.semaphore("f_step"))
            f_all = ctx.enter_context(nc.semaphore("f_all"))
            with nc.Block() as block:
                @block.vector
                def _(dve):
                    k = 0

                    def link(ins):
                        nonlocal k
                        k += 1
                        ins.then_inc(f_step, 1)
                        dve.wait_ge(f_step, k)
                    hs = STRIPS // B
                    for t, dst, op in ((tmax, ext[0], ALU.max), (tmin, ext[1], ALU.min)):
                        for h in range(2):
                            link(dve.tensor_reduce(view(dst, 0, 128, 4 * h, [[TC, TR], [1, 4]]),
                                                   view(t, 0, 128, 4 * h, [[2 * SPT * 4, TR], [1, 4], [8, SPT]]),
                                                   AX.X, op))
                        for b in range(B):
                            part = dst[:, b * TR // B * TC:(b + 1) * TR // B * TC]
                            link(dve.tensor_scalar(part, part, mean_t[:, b * hs:b * hs + 1],
                                                   rstd_t[:, STRIPS + b * hs:STRIPS + b * hs + 1],
                                                   ALU.subtract, ALU.mult))
                    link(dve.scalar_tensor_tensor(ext[0][:], ext[1][:], -1.0, ext[0][:], ALU.mult, ALU.max))
                    dve.wait_ge(f_all, 1)
                    link(dve.tensor_scalar(tabs[:], tabs[:], THRESHOLD, None, ALU.is_gt))
                    S8 = CSTRIPS * TC
                    for q in range(SPT):
                        for b in range(B):
                            n = TR // B
                            link(dve.tensor_scalar(view(ctab, 0, 128, S8 + (b * n * SPT + q) * TC, [[SPT * TC, n], [1, TC]]),
                                                   view(tabs, 0, 128, b * n * TC, [[TC, n], [1, TC]]),
                                                   rstd_t[:, STRIPS + b * hs:STRIPS + b * hs + 1], None, ALU.mult))
                    link(dve.tensor_copy(ctab[:, TC:S8], ctab[:, S8:2 * S8 - TC]))
                    link(dve.tensor_copy(ctab[:, 2 * S8:3 * S8 - TC], ctab[:, S8 + TC:2 * S8]))
                    for b in range(B):
                        link(dve.memset(ctab[:, b * S8 // B:b * S8 // B + TC], 0.0))
                        link(dve.memset(ctab[:, 2 * S8 + (b + 1) * S8 // B - TC:2 * S8 + (b + 1) * S8 // B], 0.0))

                @block.gpsimd
                def _(pool):
                    pool.wait_ge(f_step, 9)
                    pool.partition_all_reduce(tabs[:], ext[0][:], 128, RMAX).then_inc(f_all, 1)

        with ExitStack() as pc:
            names = ("zf_done", "t_done", "th_done", "tl_done", "conv_mm", "e_done", "ab_done", "sd_done",
                     "out_done", "pads", "edges")
            sem = {n: pc.enter_context(nc.semaphore(f"c_{n}")) for n in names}
            CZ = CROWS + 2
            XR = 4
            x_loaded = [pc.enter_context(nc.semaphore(f"c_x_loaded{r}")) for r in range(XR)]
            stored = [pc.enter_context(nc.semaphore(f"c_stored{r}")) for r in range(2)]
            TF, TZ = PAIRROWS * W, PAIRROWS * CW
            xc = sb("xc", XR * CZ * W, F32, pc)
            cf = sb("cf", 2 * CZ * W, F32, pc)
            tf = sb("tf", NM * TF, F32, pc)
            th, tl = sb("th", 2 * NM * TZ, F16, pc), sb("tl", 2 * NM * TZ, F16, pc)
            e12 = sb("e12", 2 * 512, F32, pc)
            sd = sb("sd", 2 * 512, F32, pc)
            oc = sb("oc", 2 * CROWS * W, F32, pc)
            zrow = sb("zrow", W, F32, pc)
            ps_c = pc.enter_context(nc.psum_tensor("ps_c", [128, 2 * NM * 512], F32))

            CFIRST, CTURNS = 5, 14

            def strips(eng, body):
                for j in range(-3, CFIRST):
                    body(j, j // XR, j % XR, lambda v: 0 <= v < CSTRIPS)
                with eng.Fori(0, CTURNS) as i:
                    for c in range(XR):
                        body(i * XR + (CFIRST + c), i + (CFIRST + c) // XR, (CFIRST + c) % XR, lambda v: True)
                for j in range(CFIRST + XR * CTURNS, CSTRIPS + 1):
                    body(j, j // XR, j % XR, lambda v: 0 <= v < CSTRIPS)

            block = pc.enter_context(nc.Block())

            @block.sync
            def _(sp):
                sp.wait_ge(sem["pads"], 1)
                sp.dma_start(x1_dram[:, 0:1, :].rearrange("p a b -> p (a b)"), zrow[:]).then_inc(sem["edges"], 16)
                sp.dma_start(x1_dram[:, ROWS + 1:ROWS + 2, :].rearrange("p a b -> p (a b)"), zrow[:]
                             ).then_inc(sem["edges"], 16)
                sp.wait_ge(sem["edges"], 32)

                def body(j, t, slot, on):
                    if on(j + 3):
                        row = settled(sp, (j + 3) * CROWS)
                        need(sp, sem["ab_done"], j * 2)
                        r = (slot + 3) % XR
                        sp.dma_start(xc[:, r * CZ * W:(r + 1) * CZ * W],
                                     x1_dram[:, bass.ds(row, CZ), :].rearrange("p a b -> p (a b)")
                                     ).then_inc(x_loaded[r], 16)
                    if on(j - 1):
                        row = settled(sp, (j - 1) * CROWS)
                        sp.wait_ge(sem["out_done"], j * 2)
                        o = (slot - 1) % 2
                        sp.dma_start(out[:, bass.ds(row, CROWS), :].rearrange("p a b -> p (a b)"),
                                     oc[:, o * CROWS * W:(o + 1) * CROWS * W]).then_inc(stored[o], 16)
                strips(sp, body)
                for done in stored:
                    sp.wait_ge(done, CSTRIPS // 2 * 16)

            @block.tensor
            def _(pe):
                def body(j, t, slot, on):
                    if not on(j):
                        return
                    pe.wait_ge(sem["tl_done"], (j + 1) * NM)
                    for half in range(2):
                        need(pe, sem["e_done"], (j - 1) * 2 + half + 1)
                        need(pe, sem["ab_done"], (j - 1) * 2 + half + 1)
                        for m in range(NM):
                            m_at = ps_c[:, (half * NM + m) * 512:(half * NM + m + 1) * 512]
                            k = 0
                            for kx in range(3):
                                t_at = lambda z: view(z, 0, 128, (slot % 2) * NM * TZ + m * TZ + 2 * half * CW + kx,
                                                      [[CW, 2], [1, W]])
                                tap = slice((m * 3 + kx) * C, (m * 3 + kx + 1) * C)
                                for wt, z in ((wc_h, th), (wc_h, tl), (wc_l, th)):
                                    last = pe.matmul(m_at, wt[:, tap], t_at(z), start=(k == 0), stop=(k == 8))
                                    k += 1
                        last.then_inc(sem["conv_mm"], 1)
                strips(pe, body)

            @block.scalar
            def _(act):
                def evict(k, half):
                    act.wait_ge(sem["conv_mm"], k + 1)
                    need(act, sem["sd_done"], k)
                    act.activation(e12[:, 0:512], ps_c[:, (half * NM + 1) * 512:(half * NM + 2) * 512],
                                   ACT.Identity, bias=bias[:, 0:1], scale=wscale[:, 2:3])
                    act.activation(e12[:, 512:1024], ps_c[:, (half * NM + 2) * 512:(half * NM + 3) * 512],
                                   ACT.Copy, scale=wscale[:, 2:3]).then_inc(sem["e_done"], 1)

                def body(j, t, slot, on):
                    if on(j - 1):
                        evict(j * 2 - 1, 1)
                    if on(j + 1):
                        need(act, sem["conv_mm"], j * 2)
                        for m in range(NM):
                            if m == 3 and on(j):
                                evict(j * 2, 0)
                            act.wait_ge(sem["t_done"], (j + 1) * NM + m + 1)
                            act.copy(view(th, 0, 128, ((slot + 1) % 2) * NM * TZ + m * TZ + 1, [[CW, PAIRROWS], [1, W]]),
                                     view(tf, 0, 128, m * TF, [[W, PAIRROWS], [1, W]])).then_inc(sem["th_done"], 1)
                    elif on(j):
                        evict(j * 2, 0)
                strips(act, body)

            @block.vector
            def _(dve):
                dve.memset(zrow[:], 0.0)
                for z in (th, tl):
                    last = dve.memset(view(z, 0, 128, 0, [[CW, 2 * NM * PAIRROWS], [CW - 1, 2]]), 0.0)
                last.then_inc(sem["pads"], 1)

                def rows_of(t, at, half, low):
                    return view(t, 0, 128, at + (4 * half + low) * W, [[2 * W, 2], [1, W]])

                def add_outer(k, half, strip_slot):
                    dve.wait_ge(sem["conv_mm"], k + 1)
                    o, r = (strip_slot % 2) * CROWS * W, (strip_slot % XR) * CZ * W + W
                    for low, m, scale in ((0, 0, wscale[:, 2:3]), (1, 3, wneg[:, 0:1])):
                        last = dve.scalar_tensor_tensor(rows_of(oc, o, half, low),
                                                        view(ps_c, 0, 128, (half * NM + m) * 512, [[W, 2], [1, W]]),
                                                        scale, rows_of(xc, r, half, low), ALU.mult, ALU.add)
                    last.then_inc(sem["ab_done"], 1)

                def add_inner(k, half, strip_slot):
                    dve.wait_ge(sem["ab_done"], k + 1)
                    dve.wait_ge(sem["sd_done"], k + 1)
                    o = (strip_slot % 2) * CROWS * W
                    for low in range(2):
                        last = dve.tensor_tensor(rows_of(oc, o, half, low), rows_of(oc, o, half, low),
                                                 view(sd, 0, 128, low * 512, [[W, 2], [1, W]]), ALU.add)
                    last.then_inc(sem["out_done"], 1)

                def normalise(j, t, slot):
                    need(dve, sem["t_done"], (j + 1) * NM)
                    dve.wait_ge(x_loaded[(slot + 2) % XR], (t + (slot + 2) // XR + 1) * 16)
                    r, c0 = ((slot + 2) % XR) * CZ * W, (slot % 2) * CZ * W
                    pos, end = (slot + 2) % SPT, CZ - 1
                    for part, r0, rn in {0: ((0, 0, 1), (1, 1, end)), SPT - 1: ((1, 0, end), (2, end, 1))}.get(
                            pos, ((1, 0, CZ),)):
                        for tc in range(TC):
                            dims, off = [[W, rn], [1, TILE]], r0 * W + tc * TILE
                            last = dve.tensor_scalar(view(cf, 0, 128, c0 + off, dims), view(xc, 0, 128, r + off, dims),
                                                     mean_t[:, bass.ds(j + 2, 1)],
                                                     ctab[:, bass.ds((j + 2) * TC + part * CSTRIPS * TC + tc, 1)],
                                                     ALU.subtract, ALU.mult)
                    last.then_inc(sem["zf_done"], 1)

                def body(j, t, slot, on):
                    if on(j - 1):
                        add_outer(j * 2 - 1, 1, slot - 1)
                    if on(j + 2):
                        normalise(j, t, slot)
                    for m in range(NM):
                        if m == 1 and on(j - 1):
                            add_inner(j * 2 - 1, 1, slot - 1)
                        if m == 3 and on(j):
                            need(dve, stored[slot % 2], (t * 2 + slot // 2) * 16)
                            add_outer(j * 2, 0, slot)
                        if on(j + 1):
                            dve.wait_ge(sem["th_done"], (j + 1) * NM + m + 1)
                            at = ((slot + 1) % 2) * NM * TZ + m * TZ + 1
                            dve.tensor_tensor(view(tl, 0, 128, at, [[CW, PAIRROWS], [1, W]]),
                                              view(tf, 0, 128, m * TF, [[W, PAIRROWS], [1, W]]),
                                              view(th, 0, 128, at, [[CW, PAIRROWS], [1, W]]), ALU.subtract
                                              ).then_inc(sem["tl_done"], 1)
                    if on(j):
                        add_inner(j * 2, 0, slot)
                strips(dve, body)

            @block.gpsimd
            def _(pool):
                OPS = ((0, 2, ALU.subtract), (1, 2, ALU.add), (2, 1, ALU.subtract), (1, 3, ALU.subtract))

                def combine(k):
                    pool.wait_ge(sem["e_done"], k + 1)
                    need(pool, sem["out_done"], k)
                    pool.tensor_tensor(sd[:, 0:512], e12[:, 0:512], e12[:, 512:1024], ALU.add)
                    pool.tensor_tensor(sd[:, 512:1024], e12[:, 0:512], e12[:, 512:1024], ALU.subtract
                                       ).then_inc(sem["sd_done"], 1)

                def body(j, t, slot, on):
                    c0 = ((slot + 1) % 2) * CZ * W
                    for m, (ra, rb, op) in enumerate(OPS):
                        if m == 1 and on(j - 1):
                            combine(j * 2 - 1)
                        if on(j + 1):
                            pool.wait_ge(sem["zf_done"], j + 2)
                            need(pool, sem["tl_done"], j * NM + m + 1)
                            pool.tensor_tensor(tf[:, m * TF:(m + 1) * TF],
                                               view(cf, 0, 128, c0 + ra * W, [[2 * W, PAIRROWS], [1, W]]),
                                               view(cf, 0, 128, c0 + rb * W, [[2 * W, PAIRROWS], [1, W]]), op
                                               ).then_inc(sem["t_done"], 1)
                    if on(j):
                        combine(j * 2)
                strips(pool, body)


def kernel(x, L0_conv_W_qkv, L0_conv_W_out, L0_conv_rel_height, L0_conv_rel_width, L1_conv_weight, L1_conv_bias):
    import numpy as np
    import concourse.bacc as bacc
    from concourse.bass_utils import run_bass_kernel_spmd

    nc = bacc.Bacc("TRN2", target_bir_lowering=False, num_devices=1)
    x = np.asarray(x)
    rows = np.zeros((C, ROWS + 2 * PAD, W), x.dtype)
    rows[:, PAD:PAD + ROWS] = x.transpose(1, 0, 2, 3).reshape(C, ROWS, W)
    lo, hi = WS + 2 * PAD - WS + 1, 2 * (WS + 2 * PAD) - 2
    rel = np.concatenate([np.asarray(t)[lo:hi:2].T for t in (L0_conv_rel_height, L0_conv_rel_width)], axis=1)
    rel = np.tile(rel, (HEADS, 1))
    part = np.arange(128)
    groups = (part[:, None] // GROUP == part[None, :] // GROUP).astype(np.float32)
    shift = np.concatenate([(QS - 1 - part[:, None] % QS == np.arange(QS)),
                            (QS - 1 - (part[:, None] // QS) % QS == np.arange(QS))], axis=1).astype(np.float32)
    first = np.tile((np.arange(STRIPS) % (STRIPS // B) != 0), (128, 1))
    final = np.tile((np.arange(STRIPS) % (STRIPS // B) != STRIPS // B - 1), (128, 1))
    arrays = {
        "rows": rows,
        "wqkv": np.ascontiguousarray(np.asarray(L0_conv_W_qkv).T),
        "wout": np.ascontiguousarray(np.asarray(L0_conv_W_out).T),
        "rel": np.ascontiguousarray(rel),
        "wconv": np.ascontiguousarray(np.asarray(L1_conv_weight).transpose(1, 2, 3, 0).reshape(C, 9 * C)),
        "bias": np.ascontiguousarray(np.asarray(L1_conv_bias).reshape(C, 1)),
        "ident": np.eye(128, dtype=np.float16),
        "groups": groups,
        "heads": (part[:, None] // DH == np.arange(HEADS)).astype(np.float16),
        "shift": shift,
        "edge": np.concatenate([first, final], axis=1).astype(np.float32),
    }
    aps = [nc.dram_tensor(n, a.shape, mybir.dt.from_np(a.dtype), kind="ExternalInput").ap() for n, a in arrays.items()]
    x1 = nc.dram_tensor("x1", (C, ROWS + 2, W), F32, kind="Internal").ap()
    out = nc.dram_tensor("out", (C, ROWS, W), F32, kind="ExternalOutput").ap()
    conv_preact_program(nc, *aps, x1, out)
    got = run_bass_kernel_spmd(nc, [arrays], core_ids=[0]).results[0]["out"]
    return np.ascontiguousarray(got.reshape(C, B, H, W).transpose(1, 0, 2, 3))
```
